# Optimizing a Trainium2 kernel written in Bass

```python
import numpy as np
import jax
import jax.numpy as jnp

def _softmax(x, axis=-1):
    return jax.nn.softmax(x, axis=axis)

def _gelu(x):
    return jax.nn.gelu(x, approximate=True)

def _silu(x):
    return jax.nn.silu(x)

def _sigmoid(x):
    return jax.nn.sigmoid(x)

def _layernorm(x, axis=-1, eps=1e-05):
    m = jnp.mean(x, axis=axis, keepdims=True)
    v = jnp.var(x, axis=axis, keepdims=True)
    return (x - m) / jnp.sqrt(v + eps)

def _scatter_add(tgt, idx, src, axis=0):
    return tgt.at[idx].add(src)

def _segment_sum(src, seg, n):
    return jax.ops.segment_sum(src, seg, n)
kernel_name = 'mk_xattn_seq_d4_seqx_r4_b50891'

def setup_inputs(seed: int=0):
    np.random.seed(seed)
    _w = jnp.asarray

    def _rec_inputs():
        import jax
        import jax.numpy as jnp
        _rk = jax.random.key(seed)
        x = -0.0002928 + 1 * jax.random.normal(jax.random.fold_in(_rk, 1), (128, 128, 256), jnp.float32)
        _lenS = 128 - jax.random.randint(jax.random.fold_in(_rk, 7), (128,), 0, max(1, 128 // 4) + 1, jnp.int32)
        _lenS2 = 128 - jax.random.randint(jax.random.fold_in(_rk, 8), (128,), 0, max(1, 128 // 4) + 1, jnp.int32)
        _ctx_1024P = jax.random.normal(jax.random.fold_in(_rk, 11), (128, 16, 256), jnp.float32)
        _ctx_1024c = jax.random.dirichlet(jax.random.fold_in(_rk, 511), 0.3 * jnp.ones((16,), jnp.float32), (128, 128))
        _ctx_1024t = jnp.einsum('bsk,bkd->bsd', _ctx_1024c, _ctx_1024P)
        _ctx_1024t = _ctx_1024t * jax.lax.rsqrt(jnp.mean(jnp.square(_ctx_1024t)) + 1e-12) * 0.953939
        ctx_1024 = -1.39393e-06 + 0.999914 * (_ctx_1024t + 0.3 * jax.random.normal(jax.random.fold_in(_rk, 611), (128, 128, 256), jnp.float32))
        itok_BxS2_4_31999 = jax.random.randint(jax.random.fold_in(_rk, 12), (128, 128), 4, 8000, jnp.int32)
        _ctxb_2048x64P = jax.random.normal(jax.random.fold_in(_rk, 13), (128, 16, 64), jnp.float32)
        _ctxb_2048x64c = jax.random.dirichlet(jax.random.fold_in(_rk, 513), 0.3 * jnp.ones((16,), jnp.float32), (128, 128))
        _ctxb_2048x64t = jnp.einsum('bsk,bkd->bsd', _ctxb_2048x64c, _ctxb_2048x64P)
        _ctxb_2048x64t = _ctxb_2048x64t * jax.lax.rsqrt(jnp.mean(jnp.square(_ctxb_2048x64t)) + 1e-12) * 0.953939
        ctxb_2048x64 = 0.50053 + 0.288505 * (_ctxb_2048x64t + 0.3 * jax.random.normal(jax.random.fold_in(_rk, 613), (128, 128, 64), jnp.float32))
        return (x, ctx_1024, itok_BxS2_4_31999, ctxb_2048x64)
    x, ctx_1024, itok_BxS2_4_31999, ctxb_2048x64 = _rec_inputs()

    def _L0_xattn_setup():
        import jax, jax.numpy as jnp
        import numpy as np
        EPS = 1e-05

        def _layernorm(x, g, b):
            m = jnp.mean(x, axis=-1, keepdims=True)
            v = jnp.mean((x - m) ** 2, axis=-1, keepdims=True)
            return (x - m) / jnp.sqrt(v + EPS) * g + b

        def _mha(x, kv, Wq, Wk, Wv, mask, causal):
            m = mask[:, None]
            Q = jnp.einsum('bsd,hdk->bhsk', x, Wq) * m
            K = jnp.einsum('bsd,hdk->bhsk', kv, Wk) * m
            V = jnp.einsum('bsd,hdk->bhsk', kv, Wv) * m
            energy = jnp.einsum('bhsk,bhtk->bhst', Q, K)
            S = energy.shape[-1]
            lengths = jnp.sum(energy[:, :, 0, :] != 0, axis=-1)
            cols = jnp.arange(S)
            energy = jnp.where(cols[None, None, None, :] >= lengths[:, :, None, None], -jnp.inf, energy)
            if causal:
                energy = jnp.where(cols[None, :] > cols[:, None], -jnp.inf, energy)
            dk = Wq.shape[-1]
            score = jax.nn.softmax(energy / jnp.sqrt(jnp.asarray(dk, energy.dtype)), axis=-1)
            out = jnp.einsum('bhst,bhtk->bhsk', score, V) * m
            B, H, Sx, dkk = out.shape
            return out.transpose(0, 2, 1, 3).reshape(B, Sx, H * dkk)
        key = jax.random.key(seed)
        ks = jax.random.split(key, 20)
        B, S, D, H = (2, 512, 256, 16)
        dk = D // H
        sd = 0.02
        inp = {'x': jax.random.normal(ks[0], (B, S, D), jnp.float32), 'context': jax.random.normal(ks[1], (B, S, D), jnp.float32), 'Wq1': jax.random.normal(ks[2], (H, D, dk), jnp.float32) * sd, 'Wk1': jax.random.normal(ks[3], (H, D, dk), jnp.float32) * sd, 'Wv1': jax.random.normal(ks[4], (H, D, dk), jnp.float32) * sd, 'Wq2': jax.random.normal(ks[5], (H, D, dk), jnp.float32) * sd, 'Wk2': jax.random.normal(ks[6], (H, D, dk), jnp.float32) * sd, 'Wv2': jax.random.normal(ks[7], (H, D, dk), jnp.float32) * sd, 'ln1_g': jnp.ones((D,), jnp.float32), 'ln1_b': jnp.zeros((D,), jnp.float32), 'ln2_g': jnp.ones((D,), jnp.float32), 'ln2_b': jnp.zeros((D,), jnp.float32), 'ln3_g': jnp.ones((D,), jnp.float32), 'ln3_b': jnp.zeros((D,), jnp.float32), 'fc1_w': jax.random.normal(ks[8], (D, D), jnp.float32) * sd, 'fc1_b': jnp.zeros((D,), jnp.float32), 'fc2_w': jax.random.normal(ks[9], (D, D), jnp.float32) * sd, 'fc2_b': jnp.zeros((D,), jnp.float32)}
        return inp
    _L0_xattn_all = _L0_xattn_setup()
    _L0_xattn_in = {k: v for k, v in _L0_xattn_all.items() if k in ('Wq1', 'Wk1', 'Wv1', 'Wq2', 'Wk2', 'Wv2', 'ln1_g', 'ln1_b', 'ln2_g', 'ln2_b', 'ln3_g', 'ln3_b', 'fc1_w', 'fc1_b', 'fc2_w', 'fc2_b')}
    del _L0_xattn_all

    def _L1_xattn_setup():
        import jax, jax.numpy as jnp
        import numpy as np
        EMBED_DIM = 256
        LN_EPS = 1e-05

        def _layernorm(x, w, b):
            m = jnp.mean(x, axis=-1, keepdims=True)
            v = jnp.mean(jnp.square(x - m), axis=-1, keepdims=True)
            return (x - m) * jax.lax.rsqrt(v + LN_EPS) * w + b

        def _attention(q, k, v, scale):
            scores = jnp.einsum('bqd,bkd->bqk', q, k) * scale
            probs = jax.nn.softmax(scores, axis=-1)
            return jnp.einsum('bqk,bkd->bqd', probs, v)
        key = jax.random.key(seed)
        ks = jax.random.split(key, 16)
        B, SQ, SK, D, H = (8, 577, 13271, EMBED_DIM, 4)
        return {'input_features': jax.random.normal(ks[0], (B, SK, D), jnp.float32), 'query_feature': jax.random.normal(ks[1], (B, SQ, D), jnp.float32), 'norm1_w': jax.random.uniform(ks[2], (D,), jnp.float32, 0.5, 1.5), 'norm1_b': jax.random.normal(ks[3], (D,), jnp.float32) * 0.1, 'norm2_w': jax.random.uniform(ks[4], (D,), jnp.float32, 0.5, 1.5), 'norm2_b': jax.random.normal(ks[5], (D,), jnp.float32) * 0.1, 'norm3_w': jax.random.uniform(ks[6], (D,), jnp.float32, 0.5, 1.5), 'norm3_b': jax.random.normal(ks[7], (D,), jnp.float32) * 0.1, 'gamma1': jax.random.uniform(ks[8], (D,), jnp.float32, 0.5, 1.5), 'gamma2': jax.random.uniform(ks[9], (D,), jnp.float32, 0.5, 1.5), 'fc1_w': jax.random.normal(ks[10], (H, D), jnp.float32) * (1.0 / np.sqrt(D)), 'fc1_b': jax.random.normal(ks[11], (H,), jnp.float32) * 0.01, 'fc2_w': jax.random.normal(ks[12], (D, H), jnp.float32) * (1.0 / np.sqrt(H)), 'fc2_b': jax.random.normal(ks[13], (D,), jnp.float32) * 0.01}
    _L1_xattn_all = _L1_xattn_setup()
    _L1_xattn_in = {k: v for k, v in _L1_xattn_all.items() if k in ('norm1_w', 'norm1_b', 'norm2_w', 'norm2_b', 'norm3_w', 'norm3_b', 'gamma1', 'gamma2', 'fc1_w', 'fc1_b', 'fc2_w', 'fc2_b')}
    del _L1_xattn_all

    def _L2_xattn_setup():
        import jax, jax.numpy as jnp
        import numpy as np
        B, SR, SF, D = (8, 512, 512, 256)
        key = jax.random.key(seed)
        k1, k2 = jax.random.split(key)
        H_real = jax.random.normal(k1, (B, SR, D), dtype=jnp.float32)
        H_fake = jax.random.normal(k2, (B, SF, D), dtype=jnp.float32)
        return {'H_real': H_real, 'H_fake': H_fake}
    _L2_xattn_all = _L2_xattn_setup()
    _L2_xattn_in = {k: v for k, v in _L2_xattn_all.items() if k in ()}
    del _L2_xattn_all

    def _L3_xattn_setup():
        import jax, jax.numpy as jnp
        import numpy as np
        BATCH, T, H, S, P, NH = (4, 512, 256, 64, 64, 8)
        HD = H // NH

        def _layernorm(x, g, b):
            mu = jnp.mean(x, axis=-1, keepdims=True)
            var = jnp.mean((x - mu) ** 2, axis=-1, keepdims=True)
            return (x - mu) * jax.lax.rsqrt(var + 1e-05) * g + b

        def _mha(q_in, kv_in, W_qkv, b_qkv, W_o, b_o):
            Wq, Wk, Wv = jnp.split(W_qkv, 3, axis=0)
            bq, bk, bv = jnp.split(b_qkv, 3, axis=0)

            def heads(x, W, b):
                y = x @ W.T + b
                return y.reshape(y.shape[0], y.shape[1], NH, HD).transpose(0, 2, 1, 3)
            q, k, v = (heads(q_in, Wq, bq), heads(kv_in, Wk, bk), heads(kv_in, Wv, bv))
            scores = jnp.einsum('bhqd,bhkd->bhqk', q, k) * (1.0 / np.sqrt(HD))
            attn = jax.nn.softmax(scores, axis=-1)
            out = jnp.einsum('bhqk,bhkd->bhqd', attn, v)
            out = out.transpose(0, 2, 1, 3).reshape(q_in.shape)
            return out @ W_o.T + b_o
        key = jax.random.key(seed)
        ks = jax.random.split(key, 16)
        sH = 1.0 / np.sqrt(H)
        d = {}
        d['builder_state'] = jax.random.normal(ks[0], (BATCH, T, H), jnp.float32)
        d['base_state'] = jax.random.normal(ks[1], (BATCH, T, H), jnp.float32)
        d['input_ids'] = jax.random.randint(ks[2], (BATCH, T), 0, 8000)
        d['program_probs'] = jax.random.uniform(ks[3], (BATCH, T, P), jnp.float32)
        d['A'] = jax.random.normal(ks[4], (S, S), jnp.float32) * (0.5 / np.sqrt(S))
        d['Bmat'] = jax.random.normal(ks[5], (H, S), jnp.float32) * sH
        d['Cmat'] = jax.random.normal(ks[6], (S, H), jnp.float32) * (1.0 / np.sqrt(S))
        d['W_in'] = jax.random.normal(ks[7], (H, H), jnp.float32) * sH
        d['b_in'] = jnp.zeros((H,), jnp.float32)
        d['W_qkv'] = jax.random.normal(ks[8], (3 * H, H), jnp.float32) * sH
        d['b_qkv'] = jnp.zeros((3 * H,), jnp.float32)
        d['W_o'] = jax.random.normal(ks[9], (H, H), jnp.float32) * sH
        d['b_o'] = jnp.zeros((H,), jnp.float32)
        d['W_prog'] = jax.random.normal(ks[10], (H, P), jnp.float32) * (1.0 / np.sqrt(P))
        d['b_prog'] = jnp.zeros((H,), jnp.float32)
        d['g1'] = jnp.ones((H,), jnp.float32)
        d['beta1'] = jnp.zeros((H,), jnp.float32)
        d['g2'] = jnp.ones((H,), jnp.float32)
        d['beta2'] = jnp.zeros((H,), jnp.float32)
        return d
    _L3_xattn_all = _L3_xattn_setup()
    _L3_xattn_in = {k: v for k, v in _L3_xattn_all.items() if k in ('A', 'Bmat', 'Cmat', 'W_in', 'b_in', 'W_qkv', 'b_qkv', 'W_o', 'b_o', 'W_prog', 'b_prog', 'g1', 'beta1', 'g2', 'beta2')}
    del _L3_xattn_all
    return {'x': x, 'ctx_1024': ctx_1024, 'itok_BxS2_4_31999': itok_BxS2_4_31999, 'ctxb_2048x64': ctxb_2048x64, 'L0_xattn_Wq1': _L0_xattn_in['Wq1'], 'L0_xattn_Wk1': _L0_xattn_in['Wk1'], 'L0_xattn_Wv1': _L0_xattn_in['Wv1'], 'L0_xattn_Wq2': _L0_xattn_in['Wq2'], 'L0_xattn_Wk2': _L0_xattn_in['Wk2'], 'L0_xattn_Wv2': _L0_xattn_in['Wv2'], 'L0_xattn_ln1_g': _L0_xattn_in['ln1_g'], 'L0_xattn_ln1_b': _L0_xattn_in['ln1_b'], 'L0_xattn_ln2_g': _L0_xattn_in['ln2_g'], 'L0_xattn_ln2_b': _L0_xattn_in['ln2_b'], 'L0_xattn_ln3_g': _L0_xattn_in['ln3_g'], 'L0_xattn_ln3_b': _L0_xattn_in['ln3_b'], 'L0_xattn_fc1_w': _L0_xattn_in['fc1_w'], 'L0_xattn_fc1_b': _L0_xattn_in['fc1_b'], 'L0_xattn_fc2_w': _L0_xattn_in['fc2_w'], 'L0_xattn_fc2_b': _L0_xattn_in['fc2_b'], 'L1_xattn_norm1_w': _L1_xattn_in['norm1_w'], 'L1_xattn_norm1_b': _L1_xattn_in['norm1_b'], 'L1_xattn_norm2_w': _L1_xattn_in['norm2_w'], 'L1_xattn_norm2_b': _L1_xattn_in['norm2_b'], 'L1_xattn_norm3_w': _L1_xattn_in['norm3_w'], 'L1_xattn_norm3_b': _L1_xattn_in['norm3_b'], 'L1_xattn_gamma1': _L1_xattn_in['gamma1'], 'L1_xattn_gamma2': _L1_xattn_in['gamma2'], 'L1_xattn_fc1_w': _L1_xattn_in['fc1_w'], 'L1_xattn_fc1_b': _L1_xattn_in['fc1_b'], 'L1_xattn_fc2_w': _L1_xattn_in['fc2_w'], 'L1_xattn_fc2_b': _L1_xattn_in['fc2_b'], 'L3_xattn_A': _L3_xattn_in['A'], 'L3_xattn_Bmat': _L3_xattn_in['Bmat'], 'L3_xattn_Cmat': _L3_xattn_in['Cmat'], 'L3_xattn_W_in': _L3_xattn_in['W_in'], 'L3_xattn_b_in': _L3_xattn_in['b_in'], 'L3_xattn_W_qkv': _L3_xattn_in['W_qkv'], 'L3_xattn_b_qkv': _L3_xattn_in['b_qkv'], 'L3_xattn_W_o': _L3_xattn_in['W_o'], 'L3_xattn_b_o': _L3_xattn_in['b_o'], 'L3_xattn_W_prog': _L3_xattn_in['W_prog'], 'L3_xattn_b_prog': _L3_xattn_in['b_prog'], 'L3_xattn_g1': _L3_xattn_in['g1'], 'L3_xattn_beta1': _L3_xattn_in['beta1'], 'L3_xattn_g2': _L3_xattn_in['g2'], 'L3_xattn_beta2': _L3_xattn_in['beta2']}

def reference(x, ctx_1024, itok_BxS2_4_31999, ctxb_2048x64, L0_xattn_Wq1, L0_xattn_Wk1, L0_xattn_Wv1, L0_xattn_Wq2, L0_xattn_Wk2, L0_xattn_Wv2, L0_xattn_ln1_g, L0_xattn_ln1_b, L0_xattn_ln2_g, L0_xattn_ln2_b, L0_xattn_ln3_g, L0_xattn_ln3_b, L0_xattn_fc1_w, L0_xattn_fc1_b, L0_xattn_fc2_w, L0_xattn_fc2_b, L1_xattn_norm1_w, L1_xattn_norm1_b, L1_xattn_norm2_w, L1_xattn_norm2_b, L1_xattn_norm3_w, L1_xattn_norm3_b, L1_xattn_gamma1, L1_xattn_gamma2, L1_xattn_fc1_w, L1_xattn_fc1_b, L1_xattn_fc2_w, L1_xattn_fc2_b, L3_xattn_A, L3_xattn_Bmat, L3_xattn_Cmat, L3_xattn_W_in, L3_xattn_b_in, L3_xattn_W_qkv, L3_xattn_b_qkv, L3_xattn_W_o, L3_xattn_b_o, L3_xattn_W_prog, L3_xattn_b_prog, L3_xattn_g1, L3_xattn_beta1, L3_xattn_g2, L3_xattn_beta2):
    import jax
    import jax.numpy as jnp

    def _L0_xattn_ref(x, context, Wq1, Wk1, Wv1, Wq2, Wk2, Wv2, ln1_g, ln1_b, ln2_g, ln2_b, ln3_g, ln3_b, fc1_w, fc1_b, fc2_w, fc2_b):
        import jax, jax.numpy as jnp
        import numpy as np
        EPS = 1e-05

        def _layernorm(x, g, b):
            m = jnp.mean(x, axis=-1, keepdims=True)
            v = jnp.mean((x - m) ** 2, axis=-1, keepdims=True)
            return (x - m) / jnp.sqrt(v + EPS) * g + b

        def _mha(x, kv, Wq, Wk, Wv, mask, causal):
            m = mask[:, None]
            Q = jnp.einsum('bsd,hdk->bhsk', x, Wq) * m
            K = jnp.einsum('bsd,hdk->bhsk', kv, Wk) * m
            V = jnp.einsum('bsd,hdk->bhsk', kv, Wv) * m
            energy = jnp.einsum('bhsk,bhtk->bhst', Q, K)
            S = energy.shape[-1]
            lengths = jnp.sum(energy[:, :, 0, :] != 0, axis=-1)
            cols = jnp.arange(S)
            energy = jnp.where(cols[None, None, None, :] >= lengths[:, :, None, None], -jnp.inf, energy)
            if causal:
                energy = jnp.where(cols[None, :] > cols[:, None], -jnp.inf, energy)
            dk = Wq.shape[-1]
            score = jax.nn.softmax(energy / jnp.sqrt(jnp.asarray(dk, energy.dtype)), axis=-1)
            out = jnp.einsum('bhst,bhtk->bhsk', score, V) * m
            B, H, Sx, dkk = out.shape
            return out.transpose(0, 2, 1, 3).reshape(B, Sx, H * dkk)
        mask0 = 1.0 - jnp.all(x == 0, axis=2, keepdims=True).astype(x.dtype)
        z = _mha(x, x, Wq1, Wk1, Wv1, mask0, causal=True)
        x1 = _layernorm(x + z, ln1_g, ln1_b)
        mask1 = 1.0 - jnp.all(x1 == 0, axis=2, keepdims=True).astype(x1.dtype)
        z = _mha(x1, context, Wq2, Wk2, Wv2, mask1, causal=False)
        x2 = _layernorm(x1 + z, ln2_g, ln2_b)
        z = jnp.maximum(x2 @ fc1_w.T + fc1_b, 0.0) * mask0
        z = (z @ fc2_w.T + fc2_b) * mask0
        return _layernorm(x2 + z, ln3_g, ln3_b)

    def _L1_xattn_ref(input_features, query_feature, norm1_w, norm1_b, norm2_w, norm2_b, norm3_w, norm3_b, gamma1, gamma2, fc1_w, fc1_b, fc2_w, fc2_b):
        import jax, jax.numpy as jnp
        import numpy as np
        EMBED_DIM = 256
        LN_EPS = 1e-05

        def _layernorm(x, w, b):
            m = jnp.mean(x, axis=-1, keepdims=True)
            v = jnp.mean(jnp.square(x - m), axis=-1, keepdims=True)
            return (x - m) * jax.lax.rsqrt(v + LN_EPS) * w + b

        def _attention(q, k, v, scale):
            scores = jnp.einsum('bqd,bkd->bqk', q, k) * scale
            probs = jax.nn.softmax(scores, axis=-1)
            return jnp.einsum('bqk,bkd->bqd', probs, v)
        scale = EMBED_DIM ** (-0.5)
        norm_X = _layernorm(input_features, norm1_w, norm1_b)
        norm_F_L = _layernorm(query_feature, norm2_w, norm2_b)
        attended = _attention(norm_F_L, norm_X, norm_X, scale)
        h = jax.nn.gelu(attended @ fc1_w.T + fc1_b, approximate=False)
        cross_attended = h @ fc2_w.T + fc2_b
        norm_cross = _layernorm(cross_attended, norm3_w, norm3_b)
        self_attended = _attention(norm_cross, norm_cross, norm_cross, scale)
        skip_connect = cross_attended + gamma1 * self_attended
        return norm_F_L + gamma2 * skip_connect

    def _L2_xattn_ref(H_real, H_fake):
        import jax, jax.numpy as jnp
        import numpy as np
        B, SR, SF, D = (8, 512, 512, 256)
        scores = jnp.einsum('brd,bfd->brf', H_real, H_fake)
        weights = jax.nn.softmax(scores, axis=-1)
        context = jnp.einsum('brf,bfd->brd', weights, H_fake)
        return H_real + context

    def _L3_xattn_ref(builder_state, base_state, input_ids, program_probs, A, Bmat, Cmat, W_in, b_in, W_qkv, b_qkv, W_o, b_o, W_prog, b_prog, g1, beta1, g2, beta2):
        import jax, jax.numpy as jnp
        import numpy as np
        BATCH, T, H, S, P, NH = (4, 512, 256, 64, 64, 8)
        HD = H // NH

        def _layernorm(x, g, b):
            mu = jnp.mean(x, axis=-1, keepdims=True)
            var = jnp.mean((x - mu) ** 2, axis=-1, keepdims=True)
            return (x - mu) * jax.lax.rsqrt(var + 1e-05) * g + b

        def _mha(q_in, kv_in, W_qkv, b_qkv, W_o, b_o):
            Wq, Wk, Wv = jnp.split(W_qkv, 3, axis=0)
            bq, bk, bv = jnp.split(b_qkv, 3, axis=0)

            def heads(x, W, b):
                y = x @ W.T + b
                return y.reshape(y.shape[0], y.shape[1], NH, HD).transpose(0, 2, 1, 3)
            q, k, v = (heads(q_in, Wq, bq), heads(kv_in, Wk, bk), heads(kv_in, Wv, bv))
            scores = jnp.einsum('bhqd,bhkd->bhqk', q, k) * (1.0 / np.sqrt(HD))
            attn = jax.nn.softmax(scores, axis=-1)
            out = jnp.einsum('bhqk,bhkd->bhqd', attn, v)
            out = out.transpose(0, 2, 1, 3).reshape(q_in.shape)
            return out @ W_o.T + b_o
        residual = builder_state
        x = _layernorm(builder_state, g1, beta1)
        base_n = _layernorm(base_state, g1, beta1)
        x = residual + _mha(x, base_n, W_qkv, b_qkv, W_o, b_o)
        residual = x
        xn = _layernorm(x, g2, beta2)
        U = (xn @ W_in.T + b_in) @ Bmat

        def step(s, u_t):
            s = jax.nn.silu(s @ A.T) + u_t
            return (s, s)
        _, states = jax.lax.scan(step, jnp.zeros((builder_state.shape[0], S), U.dtype), U.transpose(1, 0, 2))
        ssm_out = jnp.einsum('tbs,sh->bth', states, Cmat)
        x = residual + ssm_out
        mod = program_probs.mean(axis=1) @ W_prog.T + b_prog
        return x + mod[:, None, :]
    x = _L0_xattn_ref(x, ctx_1024, L0_xattn_Wq1, L0_xattn_Wk1, L0_xattn_Wv1, L0_xattn_Wq2, L0_xattn_Wk2, L0_xattn_Wv2, L0_xattn_ln1_g, L0_xattn_ln1_b, L0_xattn_ln2_g, L0_xattn_ln2_b, L0_xattn_ln3_g, L0_xattn_ln3_b, L0_xattn_fc1_w, L0_xattn_fc1_b, L0_xattn_fc2_w, L0_xattn_fc2_b)
    x = _L1_xattn_ref(ctx_1024, x, L1_xattn_norm1_w, L1_xattn_norm1_b, L1_xattn_norm2_w, L1_xattn_norm2_b, L1_xattn_norm3_w, L1_xattn_norm3_b, L1_xattn_gamma1, L1_xattn_gamma2, L1_xattn_fc1_w, L1_xattn_fc1_b, L1_xattn_fc2_w, L1_xattn_fc2_b)
    x = _L2_xattn_ref(x, ctx_1024)
    x = _L3_xattn_ref(x, ctx_1024, itok_BxS2_4_31999, ctxb_2048x64, L3_xattn_A, L3_xattn_Bmat, L3_xattn_Cmat, L3_xattn_W_in, L3_xattn_b_in, L3_xattn_W_qkv, L3_xattn_b_qkv, L3_xattn_W_o, L3_xattn_b_o, L3_xattn_W_prog, L3_xattn_b_prog, L3_xattn_g1, L3_xattn_beta1, L3_xattn_g2, L3_xattn_beta2)
    return x

_drawn_inputs = setup_inputs


def setup_inputs(seed=0):
    import zlib

    import numpy as np

    out = dict(_drawn_inputs(seed))
    spreads = {'L0_xattn_ln1_g': (1.0, 0.2),
     'L0_xattn_ln1_b': (0.0, 0.1),
     'L0_xattn_ln2_g': (1.0, 0.2),
     'L0_xattn_ln2_b': (0.0, 0.1),
     'L0_xattn_ln3_g': (1.0, 0.2),
     'L0_xattn_ln3_b': (0.0, 0.1),
     'L0_xattn_fc1_b': (0.0, 0.318),
     'L0_xattn_fc2_b': (0.0, 0.1),
     'L3_xattn_b_in': (0.0, 0.1),
     'L3_xattn_b_qkv': (0.0, 0.1),
     'L3_xattn_b_o': (0.0, 0.1),
     'L3_xattn_b_prog': (0.0, 0.1),
     'L3_xattn_g1': (1.0, 0.2),
     'L3_xattn_beta1': (0.0, 0.1),
     'L3_xattn_g2': (1.0, 0.2),
     'L3_xattn_beta2': (0.0, 0.1)}
    factors = {'L0_xattn_Wq1': 7.518, 'L0_xattn_Wk1': 7.818, 'L0_xattn_Wq2': 7.54, 'L0_xattn_Wk2': 7.501}
    for name, (base, spread) in spreads.items():
        noise = np.random.default_rng([zlib.crc32(name.encode()), seed]).standard_normal(out[name].shape)
        drawn = base * np.exp(spread * noise) if base else spread * noise
        out[name] = jnp.asarray(drawn.astype(out[name].dtype))
    for name, factor in factors.items():
        out[name] = (out[name] * factor).astype(out[name].dtype)
    return out
```

```python
from contextlib import ExitStack

import numpy as np

import concourse.bass as bass
from concourse import mybir

F32 = mybir.dt.float32
BF16 = mybir.dt.bfloat16
ALU = mybir.AluOpType
ACT = mybir.ActivationFunctionType
AX = mybir.AxisListType.X

B, S, D = 128, 128, 256
G = 2
NG = B // G
W = G * S
DH = D // 128
L0_HEADS, L0_HD = 16, 16
L3_HEADS, L3_HD = 8, 32
NS, NP = 64, 64
EPS = 1e-5
BIG = 1e30
TC = 8


class Steps:

    def __init__(self, sem, names):
        self.sem, self.names, self.at = sem, names, 0
        self.total = len(names)

    def mark(self, name):
        assert self.names[self.at % self.total] == name, (name, self.names[self.at % self.total], self.names)
        self.at += 1
        return self.sem, 1

    def done(self, name, g, k=None):
        where = [n for n, x in enumerate(self.names) if x == name]
        assert where, (name, self.names)
        c = (where[-1] if k is None else where[k]) + 1
        return self.sem, g * self.total + c

    def before(self, name, g):
        return [] if isinstance(g, int) and g == 0 else [self.done(name, g - 1)]


class Arrivals:

    def __init__(self, sem, each=1):
        self.sem, self.each = sem, each

    def done(self, g):
        return self.sem, (g + 1) * (16 * self.each)

    def before(self, g):
        return [] if isinstance(g, int) and g == 0 else [(self.sem, g * (16 * self.each))]


class Ring:

    def __init__(self, buffers, order):
        self.buffers = buffers
        self.slot = {key: n % len(buffers) for n, key in enumerate(order)}
        self.last = {}

    def of(self, key):
        return self.buffers[self.slot[key]]

    def claim(self, key, i, reader, name, lag, k=None):
        s = self.slot[key]
        was = self.last.get(s)
        waits = []
        if was is not None:
            r, n, kk, lg, it = was
            waits = [r.done(n, it - lg, kk)]
        self.last[s] = (reader, name, k, lag, i)
        return self.buffers[s], waits

    def enter(self, i):
        self.last = {s: (r, n, k, lg, i - 1) for s, (r, n, k, lg, _) in self.last.items()}


UNITS = {"self_in": 0, "self_att": 1, "ctx_in": 2, "ctx_att": 2, "ffn": 3, "pair": 3,
         "real": 4, "mix_in": 4, "mix_out": 5}
LAGS = max(UNITS.values())
ENGINES = ("pe", "act", "dve", "pool")

PASSES = {
    "self": ("self_in", "self_att", L0_HEADS, L0_HD, 32),
    "ctx": ("ctx_in", "ctx_att", L0_HEADS, L0_HD, 32),
    "mix": ("mix_in", "mix_in", L3_HEADS, L3_HD, 64),
}
TILES = [(p, b, j) for p in ("self", "ctx", "mix") for b in range(G) for j in range(PASSES[p][2] // 4)]


def iteration_order():
    fill = {
        0: [("out_mix0", "mix_out"), ("out_mix1", "mix_out"), ("x1T", "ctx_in"), ("mix_norm0", "mix_out")],
        1: [("kv3", "mix_in"), ("mix_norm1", "mix_out"), ("x4T", "real")],
        2: [("cT", "ctx_in"), ("x2T", "ffn")],
        3: [("qkv_ctx", "ctx_in"), ("kbd_ctx", "ctx_in"), ("load_again", "self_att"), ("sc_real", "real")],
        4: [("fc1", "ffn"), ("load_ctx", "self_att"), ("attT", "mix_out"), ("load_self", "self_in")],
        5: [("e0_ctx", "ctx_in"), ("pT_real", "real"), ("fc2", "ffn")],
        6: [("oproj", "mix_out"), ("av_real", "real"), ("ln3a", "ffn"), ("load_pair", "pair")],
        7: [("len_ctx", "ctx_in"), ("ln5a", "real"), ("ln6a", "mix_out"), ("ln3b", "ffn")],
        8: [("out_self0", "self_att"), ("ln5b", "real"), ("ln6b", "mix_out"), ("lnCa", "pair")],
        9: [("back_self0", "self_att"), ("lnFa", "pair"), ("lnCb", "pair"), ("xT", "self_in")],
        10: [("lnFb", "pair"), ("copy1", "ctx_att"), ("qkv_self", "self_in"), ("h5T", "real")],
        11: [("CT", "pair"), ("kbd_self", "self_in"), ("h6T", "mix_out")],
        12: [("out_self1", "self_att"), ("q3", "mix_in"), ("FT", "pair"), ("e0_self", "self_in")],
        13: [("back_self1", "self_att"), ("vx", "pair"), ("sc1", "pair"), ("u", "mix_out")],
        14: [("ln1a", "self_att"), ("len_self", "self_in")],
        15: [("ln1b", "self_att"), ("keep_self", "self_in"), ("pT1", "pair")],
        16: [("out_ctx0", "ctx_att"), ("av1", "pair")],
        17: [("back_ctx0", "ctx_att"), ("yT", "pair")],
        18: [("cross", "pair")],
        19: [("lnNb", "pair")],
        20: [("out_ctx1", "ctx_att")],
        21: [("back_ctx1", "ctx_att"), ("ncT", "pair")],
        22: [("ln2a", "ctx_att"), ("sc2", "pair")],
        23: [("pT2", "pair"), ("ln2b", "ctx_att"), ("av2", "pair")],
    }
    seq = []
    for n in range(len(TILES) + 4):
        if n < 20:
            seq.append(("scores", PASSES[TILES[n][0]][1], TILES[n]))
        for name, unit in fill[n]:
            seq.append((name, unit, ()))
        if 1 <= n < 21:
            seq.append(("exp", PASSES[TILES[n - 1][0]][1], TILES[n - 1]))
        if 3 <= n < 23:
            seq.append(("turn", PASSES[TILES[n - 3][0]][1], TILES[n - 3]))
        if n >= 4:
            seq.append(("mix_values", PASSES[TILES[n - 4][0]][1], TILES[n - 4]))
    return seq


ORDER = iteration_order()
STEPS = {
    "self_in": {
        "pe": ("xT q k v e0 len").split(),
        "act": ("xT q k v").split(),
        "dve": ("q0 nz valid vp amax keep").split(),
        "pool": ("kbd").split(),
    },
    "self_att": {
        "pe": ("scores scores scores scores turn scores turn values scores turn values scores turn values "
                 "scores turn values turn values back turn values turn values values back").split(),
        "act": ("exp exp exp probT exp probT exp probT exp probT exp probT outT exp probT probT probT outT").split(),
        "dve": ("max centre max centre max centre max centre max centre max centre max centre max centre "
                 "recip rmask norm recip rmask norm add ln1stats ln1aggr ln1ve ln1").split(),
        "pool": ("keep ln1pow ln1gain ln1").split(),
    },
    "ctx_in": {
        "pe": ("x1T cT q k v e0 len").split(),
        "act": ("x1T cT q k v").split(),
        "dve": ("amax keep q0 nz valid vp").split(),
        "pool": ("mask kbd").split(),
    },
    "ctx_att": {
        "pe": ("scores scores scores scores turn scores turn values scores turn values scores turn values "
                 "scores turn values turn values back turn values turn values values back").split(),
        "act": ("exp x1r exp exp probT exp probT exp probT exp probT exp probT outT exp probT probT probT "
                 "outT").split(),
        "dve": ("max centre max centre max centre max centre max centre max centre max centre max centre "
                 "recip rmask norm recip rmask norm add ln2stats ln2aggr ln2ve ln2").split(),
        "pool": ("copies ln2pow ln2gain ln2").split(),
    },
    "ffn": {
        "pe": ("x2T fc1 fc2").split(),
        "act": ("x2T").split(),
        "dve": ("relu bias sum ln3stats ln3aggr ln3ve ln3").split(),
        "pool": ("copies ln3pow ln3gain ln3").split(),
    },
    "pair": {
        "pe": ("CT FT vx sc1 pT1 av1 yT cross ncT sc2 pT2 av").split(),
        "act": ("HCT FT vx exp1 exp1 pT1 gelu yT cross ncT exp2 exp2 pT2").split(),
        "dve": ("lnCstats lnCaggr lnCve lnFstats lnFaggr lnFve lnC lnF NXT mx1 nm1 rs1 a4r a4 lnNstats "
                 "lnNaggr lnNve lnN mx2 nm2 rs2 sa").split(),
        "pool": ("lnCpow lnFpow lnFgain lnF lnNpow lnNgain lnN skip gam2 x4").split(),
    },
    "real": {
        "pe": ("x4T ccT screal pTreal av h5T").split(),
        "act": ("x4T ccT expreal expreal pTreal h5T").split(),
        "dve": ("mxreal nmreal rsreal x5 ln5stats ln5aggr ln5ve ln5").split(),
        "pool": ("ln5pow").split(),
    },
    "mix_in": {
        "pe": ("k v q scores scores scores scores turn turn values turn values turn values values").split(),
        "act": ("q q exp exp exp probT exp probT probT probT").split(),
        "dve": ("k v max centre max centre max centre max centre").split(),
        "pool": ("").split(),
    },
    "mix_out": {
        "pe": ("back back attT o h6T u").split(),
        "act": ("outT outT attT h6T").split(),
        "dve": ("recip norm recip norm obias res ln6stats ln6aggr ln6ve ln6 u").split(),
        "pool": ("ln6pow").split(),
    },
}
BANKS = [
    ('scores', 'self', 0, 0), ('x1T',), ('back', 'mix', 0), ('scores', 'self', 0, 1), ('k3',), ('v3',),
    ('back', 'mix', 1), ('x4T',), ('ccT',), ('scores', 'self', 0, 2), ('cT',), ('x2T',), ('scores', 'self', 0,
    3), ('q', 'ctx'), ('k', 'ctx'), ('v', 'ctx'), ('sc', 'real'), ('turn', 'self', 0, 0), ('scores', 'self',
    1, 0), ('fc1',), ('attT',), ('turn', 'self', 0, 1), ('scores', 'self', 1, 1), ('e0', 'ctx'), ('pT',
    'real'), ('fc2',), ('turn', 'self', 0, 2), ('scores', 'self', 1, 2), ('o',), ('av', 'real'), ('turn',
    'self', 0, 3), ('scores', 'self', 1, 3), ('len', 'ctx'), ('turn', 'self', 1, 0), ('scores', 'ctx', 0, 0),
    ('turn', 'self', 1, 1), ('scores', 'ctx', 0, 1), ('back', 'self', 0), ('xT',), ('turn', 'self', 1, 2),
    ('scores', 'ctx', 0, 2), ('q', 'self'), ('k', 'self'), ('v', 'self'), ('h5T',), ('turn', 'self', 1, 3),
    ('scores', 'ctx', 0, 3), ('CT',), ('h6T',), ('turn', 'ctx', 0, 0), ('scores', 'ctx', 1, 0), ('q3',),
    ('FT',), ('e0', 'self'), ('turn', 'ctx', 0, 1), ('scores', 'ctx', 1, 1), ('back', 'self', 1), ('vx',),
    ('sc', '1'), ('u',), ('turn', 'ctx', 0, 2), ('scores', 'ctx', 1, 2), ('len', 'self'), ('turn', 'ctx', 0,
    3), ('scores', 'ctx', 1, 3), ('pT', '1'), ('turn', 'ctx', 1, 0), ('scores', 'mix', 0, 0), ('av1',),
    ('turn', 'ctx', 1, 1), ('scores', 'mix', 0, 1), ('back', 'ctx', 0), ('yT',), ('turn', 'ctx', 1, 2),
    ('scores', 'mix', 1, 0), ('cross',), ('turn', 'ctx', 1, 3), ('scores', 'mix', 1, 1), ('turn', 'mix', 0,
    0), ('turn', 'mix', 0, 1), ('back', 'ctx', 1), ('ncT',), ('turn', 'mix', 1, 0), ('sc', '2'), ('turn',
    'mix', 1, 1), ('pT', '2'), ('av', '2')
]


def waits_apart(eng, passed, *waits):
    values = [v if isinstance(v, int) else eng.to_reg(v) for _, v in waits]
    eng.wait_ge(passed, 1)
    for (sem, _), value in zip(waits, values):
        eng.wait_ge(sem, value)


def drive(eng, rings, handlers):
    def body(i, full):
        for name, unit, args in ORDER:
            if not full and not 0 <= i - UNITS[unit] < NG:
                continue
            if name in handlers:
                handlers[name](i - UNITS[unit], i, *args)

    for i in range(LAGS + 1):
        body(i, False)
    if NG > LAGS + 1:
        with eng.Fori(LAGS + 1, NG) as i:
            for r in rings:
                r.enter(i)
            body(i, True)
        for r in rings:
            r.enter(NG)
    for i in range(max(NG, LAGS + 1), NG + LAGS):
        body(i, False)


def build(nc, dram):
    x_d, ctx_d, ctxb_d, out_d, res_d, u_d = (dram[n] for n in ("x", "ctx", "ctxb", "out", "res", "u"))
    x_g, ctx_g, res_g = (t.rearrange("(g b) s d -> g s b d", b=G) for t in (x_d, ctx_d, res_d))
    u_g = u_d.rearrange("(g b) n s -> g n b s", b=G)

    with ExitStack() as ctx:
        def sb(name, shape, dt=F32):
            return ctx.enter_context(nc.sbuf_tensor(name, shape, dt))

        def sem(name):
            return ctx.enter_context(nc.semaphore(name))

        ident = sb("ident", [128, 128])
        ident_b = sb("ident_b", [128, 128], BF16)
        causal = sb("causal", [128, 4, 128], BF16)
        ones_b = sb("ones_b", [128, 128], BF16)
        head_of = sb("head_of", [128, 8])
        iota = sb("iota", [128, 1])
        half = sb("half", [128, G])
        wt = {n: sb("w_" + n, [128, DH, D]) for n in
              ("q1", "k1", "v1", "q2", "k2", "v2", "fc1", "fc2", "q3", "k3", "v3", "o3")}
        w_gate = sb("w_gate", [128, DH, 4])
        w_cross = sb("w_cross", [5, D])
        w_u = sb("w_u", [128, DH, NS])
        rows = {n: sb("row_" + n, [128, D]) for n in
                ("ln1_g", "ln1_b", "ln2_g", "ln2_b", "ln3_g", "ln3_b", "n2_w", "n2_b", "n3_w", "n3_b",
                 "gam1", "gam2", "fc2_b", "o_b", "v3_b")}
        gate_b = sb("gate_b", [128, 4])
        cols = {n: sb("col_" + n, [128, DH]) for n in ("n1_w", "n1_b", "g1", "be1", "g2", "be2", "fc1_b", "q3_b", "k3_b", "in_b")}
        u_b = sb("u_b", [NS, 1])
        mod = sb("mod", [128, D])

        nat = {n: sb(n, [128, G, D]) for n in
               ("X", "XR", "CB", "Z1", "X1", "X1r", "Z2", "X2", "X3", "CC", "HC", "NF", "CR", "NC", "X4", "X5",
                "H5", "ATT", "X6", "H6")}
        trn_all = sb("turned", [128, 19, DH, W])
        trn = {n: trn_all[:, k, :, :] for k, n in enumerate(
               ("XT", "QT1", "KT1", "X1T", "CBT", "QT2", "KT2", "X2T", "HT", "FT", "NXT", "HCT", "NCT",
                "X4T", "CCT", "H5T", "QT3", "ATTT", "H6T"))}
        kbd12 = sb("kbd12", [128, 2, DH, 8, W])
        kbd1, kbd2 = kbd12[:, 0, :, :, :], kbd12[:, 1, :, :, :]
        kbd3 = sb("kbd3", [128, DH, 4, W])
        vp1 = sb("vp1", [128, G, L0_HEADS, 32])
        vp2 = sb("vp2", [128, G, L0_HEADS, 32])
        vp3 = sb("vp3", [128, G, L3_HEADS, 64])
        vn1 = sb("vn1", [128, G, D])
        vn2 = sb("vn2", [128, G, D])
        q0 = {p: sb("q0_" + p, [128, DH * G, 8]) for p in ("self", "ctx")}
        nz = {p: sb("nz_" + p, [128, G * L0_HEADS], BF16) for p in ("self", "ctx")}
        valid = {p: sb("valid_" + p, [128, G * L0_HEADS]) for p in ("self", "ctx")}
        keep0 = [sb(f"keep0_{n}", [128, G]) for n in range(4)]
        keep1 = [sb(f"keep1_{n}", [128, G]) for n in range(2)]
        amax = {n: sb("amax_" + n, [128, G]) for n in ("self", "ctx")}
        mx = [sb(f"mx{n}", [128, 4]) for n in range(2)]
        prob = [sb(f"prob{n}", [128, 4, 128]) for n in range(4)]
        probT = [sb(f"probT{n}", [128, 4, 128]) for n in range(2)]
        outT = [sb(f"outT{n}", [128, 4, 128]) for n in range(2)]
        recip = {p: sb("recip_" + p, [128, 16]) for p in PASSES}
        LN = ("ln1", "ln2", "ln3", "lnF", "lnC", "lnN", "ln5", "ln6")
        stats = {n: sb("stats_" + n, [128, G, 6]) for n in LN}
        mv = {n: sb("mv_" + n, [128, G, 2]) for n in LN}
        ve = {n: sb("ve_" + n, [128, G]) for n in LN}
        rs = {n: sb("rs_" + n, [128, G]) for n in LN}
        vxs = sb("vxs", [128, G, 4])
        nmax = {n: sb("nmax_" + n, [128, G]) for n in ("1", "2", "real")}
        nmx = {n: sb("nmx_" + n, [128, G]) for n in ("1", "2", "real")}
        psum_ = {n: sb("rsum_" + n, [128, G]) for n in ("1", "2", "real")}
        rsum = {n: sb("rrec_" + n, [128, G]) for n in ("1", "2", "real")}
        pc = {n: sb("pc_" + n, [128, G, 128]) for n in ("1", "2", "real")}
        pct = {n: sb("pct_" + n, [128, G, 128]) for n in ("1", "2", "real")}
        a4 = sb("a4", [128, G, 4])
        y5 = sb("y5", [128, G, 5])
        y5T = sb("y5T", [5, G, 128])
        us = sb("us", [NS, G, S])

        pbank = [ctx.enter_context(nc.psum_tensor(f"bank{n}", [128, 512], F32)) for n in range(8)]

        loaded, prep, mods = sem("loaded"), sem("prep"), sem("mods")
        steps = {u: {e: Steps(sem(f"{u}_{e}"), STEPS[u][e]) for e in ENGINES} for u in UNITS}
        x_in, x_in2, ctx_in2, ctx_in3 = Arrivals(sem("x_in")), Arrivals(sem("x_in2")), Arrivals(sem("ctx_in2")), Arrivals(sem("ctx_in3"))
        res_out, u_out = Arrivals(sem("res_out")), Arrivals(sem("u_out"))
        banks = Ring(pbank[0:6], BANKS)
        obanks = Ring(pbank[6:8], [(p, b) for p in PASSES for b in range(G)])
        probs = Ring(prob, TILES)
        probsT = Ring(probT, TILES)
        outsT = Ring(outT, [(p, b) for p in PASSES for b in range(G)])
        QT = {"self": trn["QT1"], "ctx": trn["QT2"], "mix": trn["QT3"]}
        KBD = {"self": kbd1, "ctx": kbd2, "mix": kbd3}
        KT = {"self": trn["KT1"], "ctx": trn["KT2"]}
        VP = {"self": vp1, "ctx": vp2, "mix": vp3}
        VN = {"self": vn1, "ctx": vn2}
        WQKV = {"self": ("q1", "k1", "v1"), "ctx": ("q2", "k2", "v2")}
        Z = {"self": nat["Z1"], "ctx": nat["Z2"], "mix": nat["ATT"]}
        self_in, self_att, ctx_in, ctx_att, ffn, pair, real, mix_in, mix_out = (steps[u] for u in UNITS)

        def flat(t):
            return t[:].rearrange("p a b -> p (a b)")

        ctxb_sb = kbd12[:].rearrange("p k a h w -> p (k a h w)")[:, 0:S // 2 * NP].rearrange("p (s n) -> p s n", n=NP)
        w_in = nat["X"]
        b_mat = nat["CB"]
        causal_f = nat["Z1"]
        w_prog = nat["Z2"]
        msum = nat["X2"]
        msT = nat["X3"]
        beta_b = nat["CC"]
        prog_b = nat["NF"]

        with nc.Block() as block:
            @block.sync
            def _(sp):
                n = 0
                for name, t in wt.items():
                    sp.dma_start(t[:], dram["w_" + name].rearrange("(a p) n -> p a n", p=128)).then_inc(loaded, 16)
                    n += 16
                for t, src in ((w_gate[:], dram["w_gate"].rearrange("(a p) n -> p a n", p=128)),
                               (w_cross[:], dram["w_cross"]),
                               (w_in[:], dram["w_in"].rearrange("(a p) n -> p a n", p=128)),
                               (b_mat[:, :, 0:NS], dram["b_mat"].rearrange("(a p) n -> p a n", p=128)),
                               (causal_f[:, 0, 0:128], dram["causal"]),
                               (w_prog[0:NP, 0, :], dram["w_prog"]),
                               (ident[:], dram["ident"]), (head_of[:], dram["head_of"]), (iota[:], dram["iota"]),
                               (gate_b[:], dram["gate_b"].partition_broadcast(128)),
                               (prog_b[:, 0, :], dram["prog_b"].partition_broadcast(128))):
                    sp.dma_start(t, src).then_inc(loaded, 16)
                    n += 16
                for name, t in rows.items():
                    sp.dma_start(t[:], dram["row_" + name].partition_broadcast(128)).then_inc(loaded, 16)
                    n += 16
                for name, t in cols.items():
                    sp.dma_start(t[:], dram["col_" + name]).then_inc(loaded, 16)
                    n += 16
                sp.wait_ge(loaded, n)

        with nc.Block() as block:
            @block.vector
            def _(dve):
                nc.vector.tensor_copy(ident_b[:], ident[:])
                for h in range(4):
                    nc.vector.tensor_scalar(causal[:, h, :], causal_f[:, 0, 0:128], -BIG, None, ALU.mult)
                nc.vector.memset(ones_b[:], 1.0)
                nc.vector.memset(half[:], -0.5)
                nc.vector.memset(vp1[:], 0.0)
                nc.vector.memset(vp2[:], 0.0)
                nc.vector.memset(vp3[:], 0.0)
                nc.vector.memset(kbd3[:], 0.0)
                nc.vector.memset(y5[:], 1.0).then_inc(prep, 1)
                dve.wait_ge(prep, 1)
                nc.vector.memset(vp3[:, :, :, L3_HD], 1.0)
                nc.vector.tensor_copy(beta_b[:, :, 0:128], cols["be1"][:].unsqueeze(2).to_broadcast([128, DH, 128])).then_inc(prep, 1)
                dve.wait_ge(prep, 3)
                nc.vector.tensor_tensor(cols["q3_b"][:], cols["q3_b"][:], pbank[0][:, 0:2], ALU.add)
                nc.vector.tensor_tensor(cols["k3_b"][:], cols["k3_b"][:], pbank[0][:, 2:4], ALU.add)
                nc.vector.tensor_tensor(rows["v3_b"][:], rows["v3_b"][:], pbank[1][:, 0:D], ALU.add)
                nc.vector.tensor_copy(w_u[:], pbank[2][:, 0:DH * NS].rearrange("p (a n) -> p a n", a=DH)).then_inc(prep, 1)
                dve.wait_ge(prep, 5)
                nc.vector.tensor_copy(u_b[:], pbank[3][0:NS, 0:1])
                for a in range(DH):
                    for name, g in (("q3", "g1"), ("k3", "g1"), ("v3", "g1")):
                        nc.vector.tensor_scalar(wt[name][:, a, :], wt[name][:, a, :], cols[g][:, a:a + 1], None, ALU.mult)
                    last = nc.vector.tensor_scalar(w_u[:, a, :], w_u[:, a, :], cols["g2"][:, a:a + 1], None, ALU.mult)
                last.then_inc(prep, 1)
                for c in range(2):
                    dve.wait_ge(mods, 16 * (c + 1))
                    nc.vector.reduce_sum(msum[:, c, 0:NP], ctxb_sb.rearrange("p s n -> p n s"), AX).then_inc(prep, 1)
                    dve.wait_ge(prep, 7 + c)
                nc.vector.tensor_tensor(msum[:, 0, 128:128 + NP], msum[:, 0, 0:NP], msum[:, 1, 0:NP], ALU.add).then_inc(prep, 1)
                dve.wait_ge(prep, 9)
                nc.vector.tensor_scalar(msum[:, 1, 128:128 + NP], msum[:, 0, 128:128 + NP], 1.0 / S, None, ALU.mult).then_inc(prep, 1)
                dve.wait_ge(prep, 11)
                nc.vector.tensor_copy(msT[0:NP, 0, 0:128], pbank[4][0:NP, 0:128]).then_inc(prep, 1)
                dve.wait_ge(prep, 13)
                nc.vector.tensor_tensor(mod[:], pbank[5][:, 0:D], prog_b[:, 0, :], ALU.add).then_inc(prep, 1)
                dve.wait_ge(prep, 14)

            @block.sync
            def _(sp):
                ctxb_v = ctxb_d.rearrange("b (c s) n -> b c s n", c=2)
                for c in range(2):
                    if c:
                        sp.wait_ge(prep, 6 + c)
                    sp.dma_start(ctxb_sb, ctxb_v[:, c, :, :]).then_inc(mods, 16)
                sp.wait_ge(mods, 32)

            @block.tensor
            def _(pe):
                pe.wait_ge(prep, 2)
                for k, name in enumerate(("q3", "k3")):
                    for m in range(DH):
                        for a in range(DH):
                            nc.tensor.matmul(pbank[0][:, 2 * k + m:2 * k + m + 1], wt[name][:, a, m * 128:(m + 1) * 128],
                                             cols["be1"][:, a:a + 1], start=(a == 0), stop=(a == DH - 1))
                for a in range(DH):
                    nc.tensor.matmul(pbank[1][:, 0:D], beta_b[:, a, 0:128], wt["v3"][:, a, :], start=(a == 0), stop=(a == DH - 1))
                for m in range(DH):
                    for a in range(DH):
                        last = nc.tensor.matmul(pbank[2][:, m * NS:(m + 1) * NS], w_in[:, a, m * 128:(m + 1) * 128],
                                                b_mat[:, a, 0:NS], start=(a == 0), stop=(a == DH - 1))
                last.then_inc(prep, 1)
                pe.wait_ge(prep, 4)
                for a in range(DH):
                    nc.tensor.matmul(pbank[3][0:NS, 0:1], w_u[:, a, :], cols["be2"][:, a:a + 1], start=(a == 0), stop=False)
                for a in range(DH):
                    last = nc.tensor.matmul(pbank[3][0:NS, 0:1], b_mat[:, a, 0:NS], cols["in_b"][:, a:a + 1],
                                            start=False, stop=(a == DH - 1))
                last.then_inc(prep, 1)
                pe.wait_ge(prep, 10)
                nc.tensor.transpose(pbank[4][0:NP, 0:128], msum[:, 1, 128:128 + NP], ident[:]).then_inc(prep, 1)
                pe.wait_ge(prep, 12)
                nc.tensor.matmul(pbank[5][:, 0:D], msT[0:NP, 0, 0:128], w_prog[0:NP, 0, :], start=True, stop=True).then_inc(prep, 1)

        with nc.Block() as block:
            @block.sync
            def _(sp):
                def load_self(g, i):
                    waits_apart(sp, prep, *self_in["pe"].before("xT", g), *self_in["dve"].before("amax", g))
                    sp.dma_start(nat["X"][:], x_g[g]).then_inc(x_in.sem, 16)

                def load_again(g, i):
                    for w in self_att["dve"].before("add", g):
                        sp.wait_ge(*w)
                    sp.dma_start(nat["XR"][:], x_g[g]).then_inc(x_in2.sem, 16)

                def load_ctx(g, i):
                    for w in ctx_in["pe"].before("cT", g):
                        sp.wait_ge(*w)
                    sp.dma_start(nat["CB"][:], ctx_g[g]).then_inc(ctx_in2.sem, 16)

                def load_pair(g, i):
                    for w in real["pe"].before("av", g):
                        sp.wait_ge(*w)
                    sp.dma_start(nat["CC"][:], ctx_g[g]).then_inc(ctx_in3.sem, 16)

                def oproj(g, i):
                    sp.wait_ge(*mix_out["dve"].done("res", g))
                    sp.dma_start(res_g[g], nat["X6"][:]).then_inc(res_out.sem, 16)

                def u(g, i):
                    sp.wait_ge(*mix_out["dve"].done("u", g))
                    sp.dma_start(u_g[g], us[:]).then_inc(u_out.sem, 16)

                drive(sp, [], dict(load_self=load_self, load_again=load_again, load_ctx=load_ctx, load_pair=load_pair, oproj=oproj, u=u))
                sp.wait_ge(*res_out.done(NG - 1))
                sp.wait_ge(*u_out.done(NG - 1))

            @block.tensor
            def _(pe):
                def bank(key, i, reader, name, unit, k=None):
                    t, waits = banks.claim(key, i, reader, name, UNITS[unit], k)
                    for w in waits:
                        pe.wait_ge(*w)
                    return t

                def turn4(t, src):
                    for a in range(DH):
                        for b in range(G):
                            last = nc.tensor.transpose(t[:, a * W + b * S:a * W + (b + 1) * S],
                                                       src[:, b, a * 128:(a + 1) * 128], ident[:])
                    return last

                def proj_turned(t, w, src):
                    for m in range(DH):
                        for a in range(DH):
                            last = nc.tensor.matmul(t[:, m * W:(m + 1) * W], w[:, a, m * 128:(m + 1) * 128],
                                                    src[:, a, :], start=(a == 0), stop=(a == DH - 1))
                    return last

                def proj_natural(t, w, src):
                    for b in range(G):
                        for a in range(DH):
                            last = nc.tensor.matmul(t[:, b * D:(b + 1) * D], src[:, a, b * S:(b + 1) * S],
                                                    w[:, a, :], start=(a == 0), stop=(a == DH - 1))
                    return last

                def scores(g, i, p, b, j):
                    u_in, u_att = steps[PASSES[p][0]], steps[PASSES[p][1]]
                    if b == 0 and j == 0:
                        if p == "mix":
                            pe.wait_ge(*mix_in["act"].done("q", g))
                            pe.wait_ge(*mix_in["dve"].done("k", g))
                        else:
                            pe.wait_ge(*u_in["act"].done("q", g))
                            pe.wait_ge(*u_in["pool"].done("kbd", g))
                    t = bank(("scores", p, b, j), i, u_att["dve"], "centre", PASSES[p][1], TILES.index((p, b, j)) - TILES.index((p, 0, 0)))
                    a, h0 = (j // 2, 4 * (j % 2)) if p != "mix" else (j, 0)
                    if p == "self":
                        nc.tensor.matmul(t[:, :], ident_b[:], causal[:].rearrange("p h t -> p (h t)"), start=True, stop=False)
                    nc.tensor.matmul(t[:, :], QT[p][:, a, b * S:(b + 1) * S], KBD[p][:, a, h0:h0 + 4, b * S:(b + 1) * S],
                                     start=(p != "self"), stop=True).then_inc(*u_att["pe"].mark("scores"))

                def turn(g, i, p, b, j):
                    u_att = steps[PASSES[p][1]]
                    n = TILES.index((p, b, j)) - TILES.index((p, 0, 0))
                    t = bank(("turn", p, b, j), i, u_att["act"], "probT", PASSES[p][1], n)
                    pe.wait_ge(*u_att["act"].done("exp", g, n))
                    src = probs.of((p, b, j))
                    for h in range(4):
                        last = nc.tensor.transpose(t[:, h * 128:(h + 1) * 128], src[:, h, :], ident[:])
                    last.then_inc(*u_att["pe"].mark("turn"))

                def mix_values(g, i, p, b, j):
                    u_in, u_att, heads, hd, gw = steps[PASSES[p][0]], steps[PASSES[p][1]], *PASSES[p][2:]
                    n = TILES.index((p, b, j)) - TILES.index((p, 0, 0))
                    if b == 0 and j == 0:
                        if p == "mix":
                            pe.wait_ge(*mix_in["dve"].done("v", g))
                        else:
                            pe.wait_ge(*u_in["dve"].done("vp", g))
                    if j == 0:
                        reader, lag = (mix_out, "mix_out") if p == "mix" else (u_att, PASSES[p][1])
                        t, waits = obanks.claim((p, b), i, reader["act"], "outT", UNITS[PASSES[p][1]], b)
                        for w in waits:
                            pe.wait_ge(*w)
                    t = obanks.of((p, b))
                    pe.wait_ge(*u_att["act"].done("probT", g, n))
                    per = 128 // gw
                    for h4 in range(4):
                        h = 4 * j + h4
                        r, c = h % per, h // per
                        last = nc.tensor.matmul(t[r * gw:(r + 1) * gw, c * 128:(c + 1) * 128], VP[p][:, b, h, 0:gw],
                                                probsT.of((p, b, j))[:, h4, :], start=True, stop=True)
                    last.then_inc(*u_att["pe"].mark("values"))

                def back(p, b, unit):
                    def go(g, i):
                        st = steps[unit]
                        t = bank(("back", p, b), i, st["dve"], "norm", unit, b)
                        pe.wait_ge(*st["act"].done("outT", g, b))
                        for c in range(4):
                            last = nc.tensor.transpose(t[:, c * 128:(c + 1) * 128], outsT.of((p, b))[:, c, :], ident[:])
                        last.then_inc(*st["pe"].mark("back"))
                    return go

                def xT(g, i):
                    t = bank(("xT",), i, self_in["act"], "xT", "self_in")
                    pe.wait_ge(*x_in.done(g))
                    turn4(t, nat["X"]).then_inc(*self_in["pe"].mark("xT"))

                def x1T(g, i):
                    t = bank(("x1T",), i, ctx_in["act"], "x1T", "ctx_in")
                    pe.wait_ge(*self_att["pool"].done("ln1", g))
                    turn4(t, nat["X1"]).then_inc(*ctx_in["pe"].mark("x1T"))

                def cT(g, i):
                    t = bank(("cT",), i, ctx_in["act"], "cT", "ctx_in")
                    pe.wait_ge(*ctx_in["pool"].done("mask", g))
                    turn4(t, nat["CB"]).then_inc(*ctx_in["pe"].mark("cT"))

                def qkv(p, unit, src_q, src_kv, last_q, last_kv):
                    def go(g, i):
                        st = steps[unit]
                        wq, wk, wv = WQKV[p]
                        t = bank(("q", p), i, st["act"], "q", unit)
                        pe.wait_ge(*st["act"].done(last_q, g))
                        proj_turned(t, wt[wq], src_q).then_inc(*st["pe"].mark("q"))
                        t = bank(("k", p), i, st["act"], "k", unit)
                        pe.wait_ge(*st["act"].done(last_kv, g))
                        proj_turned(t, wt[wk], src_kv).then_inc(*st["pe"].mark("k"))
                        t = bank(("v", p), i, st["act"], "v", unit)
                        proj_natural(t, wt[wv], src_kv).then_inc(*st["pe"].mark("v"))
                    return go

                def e0(p, unit):
                    def go(g, i):
                        st = steps[unit]
                        t = bank(("e0", p), i, st["dve"], "nz", unit)
                        pe.wait_ge(*st["dve"].done("q0", g))
                        pe.wait_ge(*st["act"].done("k", g))
                        for b in range(G):
                            for a in range(DH):
                                c = (b * DH + a) * 8
                                last = nc.tensor.matmul(t[:, c:c + 8], KT[p][:, a, b * S:(b + 1) * S],
                                                        q0[p][:, a * G + b, :], start=True, stop=True)
                        last.then_inc(*st["pe"].mark("e0"))
                    return go

                def length(p, unit):
                    def go(g, i):
                        st = steps[unit]
                        t = bank(("len", p), i, st["dve"], "valid", unit)
                        pe.wait_ge(*st["dve"].done("nz", g))
                        nc.tensor.matmul(t[:, 0:G * L0_HEADS], ones_b[:], nz[p][:], start=True, stop=True)\
                            .then_inc(*st["pe"].mark("len"))
                    return go

                def x2T(g, i):
                    t = bank(("x2T",), i, ffn["act"], "x2T", "ffn")
                    pe.wait_ge(*ctx_att["pool"].done("ln2", g))
                    turn4(t, nat["X2"]).then_inc(*ffn["pe"].mark("x2T"))

                def fc1(g, i):
                    t = bank(("fc1",), i, ffn["dve"], "relu", "ffn")
                    pe.wait_ge(*ffn["act"].done("x2T", g))
                    proj_turned(t, wt["fc1"], trn["X2T"]).then_inc(*ffn["pe"].mark("fc1"))

                def fc2(g, i):
                    t = bank(("fc2",), i, ffn["dve"], "bias", "ffn")
                    pe.wait_ge(*ffn["dve"].done("relu", g))
                    proj_natural(t, wt["fc2"], trn["HT"]).then_inc(*ffn["pe"].mark("fc2"))

                def FT(g, i):
                    t = bank(("FT",), i, pair["act"], "FT", "pair")
                    pe.wait_ge(*pair["pool"].done("lnF", g))
                    turn4(t, nat["NF"]).then_inc(*pair["pe"].mark("FT"))

                def CT(g, i):
                    t = bank(("CT",), i, pair["dve"], "NXT", "pair")
                    pe.wait_ge(*pair["dve"].done("lnC", g))
                    turn4(t, nat["HC"]).then_inc(*pair["pe"].mark("CT"))

                def vx(g, i):
                    t = bank(("vx",), i, pair["act"], "vx", "pair")
                    pe.wait_ge(*pair["dve"].done("NXT", g))
                    for b in range(G):
                        for a in range(DH):
                            last = nc.tensor.matmul(t[:, b * 4:b * 4 + 4], trn["NXT"][:, a, b * S:(b + 1) * S],
                                                    w_gate[:, a, :], start=(a == 0), stop=(a == DH - 1))
                    last.then_inc(*pair["pe"].mark("vx"))

                def score_one(key, st, unit, qT, kT, waits):
                    def go(g, i):
                        t = bank(("sc", key), i, st["act"], "exp" + key, unit)
                        for who, name in waits:
                            pe.wait_ge(*who.done(name, g))
                        for b in range(G):
                            for a in range(DH):
                                last = nc.tensor.matmul(t[:, b * S:(b + 1) * S], qT[:, a, b * S:(b + 1) * S],
                                                        kT[:, a, b * S:(b + 1) * S], start=(a == 0), stop=(a == DH - 1))
                        last.then_inc(*st["pe"].mark("sc" + key))
                    return go

                def turn_one(key, st, unit):
                    def go(g, i):
                        t = bank(("pT", key), i, st["act"], "pT" + key, unit)
                        pe.wait_ge(*st["act"].done("exp" + key, g))
                        for b in range(G):
                            last = nc.tensor.transpose(t[:, b * S:(b + 1) * S], pc[key][:, b, :], ident[:])
                        last.then_inc(*st["pe"].mark("pT" + key))
                    return go

                def av1(g, i):
                    t = bank(("av1",), i, pair["dve"], "a4", "pair")
                    pe.wait_ge(*pair["act"].done("pT1", g))
                    for b in range(G):
                        last = nc.tensor.matmul(t[:, b * 4:b * 4 + 4], pct["1"][:, b, :], vxs[:, b, :], start=True, stop=True)
                    last.then_inc(*pair["pe"].mark("av1"))

                def yT(g, i):
                    t = bank(("yT",), i, pair["act"], "yT", "pair")
                    pe.wait_ge(*pair["act"].done("gelu", g))
                    for b in range(G):
                        last = nc.tensor.transpose(t[0:5, b * S:(b + 1) * S], y5[:, b, :], ident[:])
                    last.then_inc(*pair["pe"].mark("yT"))

                def cross(g, i):
                    t = bank(("cross",), i, pair["act"], "cross", "pair")
                    pe.wait_ge(*pair["act"].done("yT", g))
                    for b in range(G):
                        last = nc.tensor.matmul(t[:, b * D:(b + 1) * D], y5T[:, b, :], w_cross[:], start=True, stop=True)
                    last.then_inc(*pair["pe"].mark("cross"))

                def ncT(g, i):
                    t = bank(("ncT",), i, pair["act"], "ncT", "pair")
                    pe.wait_ge(*pair["pool"].done("lnN", g))
                    turn4(t, nat["NC"]).then_inc(*pair["pe"].mark("ncT"))

                def av_wide(key, st, unit, values, reader):
                    def go(g, i):
                        t = bank(("av", key), i, st["dve"], reader, unit)
                        pe.wait_ge(*st["act"].done("pT" + key, g))
                        for b in range(G):
                            last = nc.tensor.matmul(t[:, b * D:(b + 1) * D], pct[key][:, b, :], values[:, b, :],
                                                    start=True, stop=True)
                        last.then_inc(*st["pe"].mark("av"))
                    return go

                def x4T(g, i):
                    t = bank(("x4T",), i, real["act"], "x4T", "real")
                    pe.wait_ge(*pair["pool"].done("x4", g))
                    turn4(t, nat["X4"]).then_inc(*real["pe"].mark("x4T"))
                    t = bank(("ccT",), i, real["act"], "ccT", "real")
                    pe.wait_ge(*ctx_in3.done(g))
                    turn4(t, nat["CC"]).then_inc(*real["pe"].mark("ccT"))

                def h5T(g, i):
                    t = bank(("h5T",), i, real["act"], "h5T", "real")
                    pe.wait_ge(*real["dve"].done("ln5", g))
                    turn4(t, nat["H5"]).then_inc(*real["pe"].mark("h5T"))

                def kv3(g, i):
                    t = bank(("k3",), i, mix_in["dve"], "k", "mix_in")
                    pe.wait_ge(*pair["act"].done("HCT", g))
                    proj_turned(t, wt["k3"], trn["HCT"]).then_inc(*mix_in["pe"].mark("k"))
                    t = bank(("v3",), i, mix_in["dve"], "v", "mix_in")
                    proj_natural(t, wt["v3"], trn["HCT"]).then_inc(*mix_in["pe"].mark("v"))

                def q3(g, i):
                    t = bank(("q3",), i, mix_in["act"], "q", "mix_in")
                    pe.wait_ge(*real["act"].done("h5T", g))
                    proj_turned(t, wt["q3"], trn["H5T"]).then_inc(*mix_in["pe"].mark("q"))

                def attT(g, i):
                    t = bank(("attT",), i, mix_out["act"], "attT", "mix_out")
                    pe.wait_ge(*mix_out["dve"].done("norm", g))
                    turn4(t, nat["ATT"]).then_inc(*mix_out["pe"].mark("attT"))

                def oproj(g, i):
                    t = bank(("o",), i, mix_out["dve"], "obias", "mix_out")
                    pe.wait_ge(*mix_out["act"].done("attT", g))
                    proj_natural(t, wt["o3"], trn["ATTT"]).then_inc(*mix_out["pe"].mark("o"))

                def h6T(g, i):
                    t = bank(("h6T",), i, mix_out["act"], "h6T", "mix_out")
                    pe.wait_ge(*mix_out["dve"].done("ln6", g))
                    turn4(t, nat["H6"]).then_inc(*mix_out["pe"].mark("h6T"))

                def u(g, i):
                    t = bank(("u",), i, mix_out["dve"], "u", "mix_out")
                    pe.wait_ge(*mix_out["act"].done("h6T", g))
                    for a in range(DH):
                        last = nc.tensor.matmul(t[0:NS, 0:W], w_u[:, a, :], trn["H6T"][:, a, :], start=(a == 0), stop=(a == DH - 1))
                    last.then_inc(*mix_out["pe"].mark("u"))

                drive(pe, [banks, obanks], dict(
                    scores=scores, turn=turn, mix_values=mix_values,
                    back_self0=back("self", 0, "self_att"), back_self1=back("self", 1, "self_att"),
                    back_ctx0=back("ctx", 0, "ctx_att"), back_ctx1=back("ctx", 1, "ctx_att"),
                    mix_norm0=back("mix", 0, "mix_out"), mix_norm1=back("mix", 1, "mix_out"),
                    xT=xT, x1T=x1T, cT=cT,
                    qkv_self=qkv("self", "self_in", trn["XT"], trn["XT"], "xT", "xT"),
                    qkv_ctx=qkv("ctx", "ctx_in", trn["X1T"], trn["CBT"], "x1T", "cT"),
                    e0_self=e0("self", "self_in"), e0_ctx=e0("ctx", "ctx_in"),
                    len_self=length("self", "self_in"), len_ctx=length("ctx", "ctx_in"),
                    x2T=x2T, fc1=fc1, fc2=fc2, FT=FT, CT=CT, vx=vx,
                    sc1=score_one("1", pair, "pair", trn["FT"], trn["NXT"], [(pair["act"], "FT"), (pair["dve"], "NXT")]),
                    pT1=turn_one("1", pair, "pair"), av1=av1, yT=yT, cross=cross, ncT=ncT,
                    sc2=score_one("2", pair, "pair", trn["NCT"], trn["NCT"], [(pair["act"], "ncT")]),
                    pT2=turn_one("2", pair, "pair"), av2=av_wide("2", pair, "pair", nat["NC"], "sa"),
                    x4T=x4T,
                    sc_real=score_one("real", real, "real", trn["X4T"], trn["CCT"], [(real["act"], "ccT")]),
                    pT_real=turn_one("real", real, "real"), av_real=av_wide("real", real, "real", nat["CC"], "x5"), h5T=h5T, kv3=kv3, q3=q3, attT=attT, oproj=oproj, h6T=h6T, u=u))

            @block.scalar
            def _(act):
                SCALE = {"self": L0_HD ** -0.5, "ctx": L0_HD ** -0.5, "mix": L3_HD ** -0.5}

                def evac(dst, st, name, unit, key, frees, n=512):
                    def go(g, i):
                        for who, what in frees:
                            for w in who.before(what, g):
                                act.wait_ge(*w)
                        act.wait_ge(*st["pe"].done(name, g))
                        nc.scalar.activation(dst, banks.of(key)[:, 0:n], ACT.Copy).then_inc(*st["act"].mark(name))
                    return go

                def exp(g, i, p, b, j):
                    st = steps[PASSES[p][1]]
                    n = TILES.index((p, b, j)) - TILES.index((p, 0, 0))
                    act.wait_ge(*st["dve"].done("centre", g, n))
                    t = probs.of((p, b, j))
                    nc.scalar.activation(flat(t), flat(t), ACT.Exp, scale=SCALE[p]).then_inc(*st["act"].mark("exp"))

                def turn(g, i, p, b, j):
                    st = steps[PASSES[p][1]]
                    n = TILES.index((p, b, j)) - TILES.index((p, 0, 0))
                    t, waits = probsT.claim((p, b, j), i, st["pe"], "values", UNITS[PASSES[p][1]], n)
                    for w in waits:
                        act.wait_ge(*w)
                    act.wait_ge(*st["pe"].done("turn", g, n))
                    nc.scalar.activation(flat(t), banks.of(("turn", p, b, j))[:, :], ACT.Copy).then_inc(*st["act"].mark("probT"))

                def out(p, b, unit):
                    def go(g, i):
                        st = steps[unit]
                        src = steps[PASSES[p][1]]
                        t, waits = outsT.claim((p, b), i, st["pe"], "back", UNITS[unit], b)
                        for w in waits:
                            act.wait_ge(*w)
                        act.wait_ge(*src["pe"].done("values", g, (b + 1) * (PASSES[p][2] // 4) - 1))
                        nc.scalar.activation(flat(t), obanks.of((p, b))[:, :], ACT.Copy).then_inc(*st["act"].mark("outT"))
                    return go

                def copy1(g, i):
                    for w in ctx_att["dve"].before("add", g):
                        act.wait_ge(*w)
                    act.wait_ge(*self_att["pool"].done("ln1", g))
                    nc.scalar.activation(flat(nat["X1r"]), flat(nat["X1"]), ACT.Copy).then_inc(*ctx_att["act"].mark("x1r"))

                def qkv(p, unit, att):
                    def go(g, i):
                        st = steps[unit]
                        evac(flat(QT[p]), st, "q", unit, ("q", p), [(steps[att]["pe"], "scores"), (st["dve"], "q0")])(g, i)
                        evac(flat(KT[p]), st, "k", unit, ("k", p), [(st["pe"], "e0"), (st["pool"], "kbd")])(g, i)
                        evac(flat(VN[p]), st, "v", unit, ("v", p), [(st["dve"], "vp")])(g, i)
                    return go

                def CT(g, i):
                    for w in mix_in["pe"].before("v", g):
                        act.wait_ge(*w)
                    act.wait_ge(*pair["pe"].done("CT", g))
                    nc.scalar.activation(flat(trn["HCT"]), banks.of(("CT",))[:, :], ACT.Copy).then_inc(*pair["act"].mark("HCT"))

                def exp_one(key, st, scale):
                    def go(g, i):
                        for w in st["pe"].before("pT" + key, g):
                            act.wait_ge(*w)
                        for w in st["dve"].before("rs" + key, g):
                            act.wait_ge(*w)
                        act.wait_ge(*st["dve"].done("nm" + key, g))
                        for b in range(G):
                            nc.scalar.activation(pc[key][:, b, :], banks.of(("sc", key))[:, b * S:(b + 1) * S], ACT.Exp,
                                                 bias=nmax[key][:, b:b + 1], scale=scale,
                                                 accum_out=psum_[key][:, b:b + 1]).then_inc(*st["act"].mark("exp" + key))
                    return go

                def av1(g, i):
                    for w in pair["pe"].before("yT", g):
                        act.wait_ge(*w)
                    act.wait_ge(*pair["dve"].done("a4", g))
                    nc.scalar.activation(y5[:, :, 0:4], a4[:], ACT.Gelu).then_inc(*pair["act"].mark("gelu"))

                def yT(g, i):
                    for w in pair["pe"].before("cross", g):
                        act.wait_ge(*w)
                    act.wait_ge(*pair["pe"].done("yT", g))
                    nc.scalar.activation(y5T[:].rearrange("p b s -> p (b s)"), banks.of(("yT",))[0:5, 0:W], ACT.Copy)\
                        .then_inc(*pair["act"].mark("yT"))

                def x4T(g, i):
                    evac(flat(trn["X4T"]), real, "x4T", "real", ("x4T",), [(real["pe"], "screal")])(g, i)
                    evac(flat(trn["CCT"]), real, "ccT", "real", ("ccT",), [(real["pe"], "screal")])(g, i)

                def turn_one(key, st, unit, reader):
                    return evac(flat(pct[key]), st, "pT" + key, unit, ("pT", key), [(st["pe"], reader)], n=W)

                def q3(g, i):
                    for w in mix_in["pe"].before("scores", g):
                        act.wait_ge(*w)
                    act.wait_ge(*mix_in["pe"].done("q", g))
                    for a in range(DH):
                        nc.scalar.activation(trn["QT3"][:, a, :], banks.of(("q3",))[:, a * W:(a + 1) * W], ACT.Identity,
                                             bias=cols["q3_b"][:, a:a + 1]).then_inc(*mix_in["act"].mark("q"))

                drive(act, [probsT, outsT], dict(
                    exp=exp, turn=turn, copy1=copy1,
                    out_self0=out("self", 0, "self_att"), out_self1=out("self", 1, "self_att"),
                    out_ctx0=out("ctx", 0, "ctx_att"), out_ctx1=out("ctx", 1, "ctx_att"),
                    out_mix0=out("mix", 0, "mix_out"), out_mix1=out("mix", 1, "mix_out"),
                    xT=evac(flat(trn["XT"]), self_in, "xT", "self_in", ("xT",), [(self_in["pe"], "v")]),
                    x1T=evac(flat(trn["X1T"]), ctx_in, "x1T", "ctx_in", ("x1T",), [(ctx_in["pe"], "q")]),
                    cT=evac(flat(trn["CBT"]), ctx_in, "cT", "ctx_in", ("cT",), [(ctx_in["pe"], "v")]),
                    qkv_self=qkv("self", "self_in", "self_att"), qkv_ctx=qkv("ctx", "ctx_in", "ctx_att"),
                    x2T=evac(flat(trn["X2T"]), ffn, "x2T", "ffn", ("x2T",), [(ffn["pe"], "fc1")]),
                    FT=evac(flat(trn["FT"]), pair, "FT", "pair", ("FT",), [(pair["pe"], "sc1")]),
                    CT=CT,
                    vx=evac(flat(vxs), pair, "vx", "pair", ("vx",), [(pair["pe"], "av1")], n=G * 4),
                    sc1=exp_one("1", pair, D ** -0.5), pT1=turn_one("1", pair, "pair", "av1"), av1=av1, yT=yT,
                    cross=evac(flat(nat["CR"]), pair, "cross", "pair", ("cross",), [(pair["pool"], "skip")]),
                    ncT=evac(flat(trn["NCT"]), pair, "ncT", "pair", ("ncT",), [(pair["pe"], "sc2")]),
                    sc2=exp_one("2", pair, D ** -0.5), pT2=turn_one("2", pair, "pair", "av"),
                    x4T=x4T, sc_real=exp_one("real", real, 1.0), pT_real=turn_one("real", real, "real", "av"),
                    h5T=evac(flat(trn["H5T"]), real, "h5T", "real", ("h5T",), [(mix_in["pe"], "q")]),
                    q3=q3,
                    attT=evac(flat(trn["ATTT"]), mix_out, "attT", "mix_out", ("attT",), [(mix_out["pe"], "o")]),
                    h6T=evac(flat(trn["H6T"]), mix_out, "h6T", "mix_out", ("h6T",), [(mix_out["pe"], "u")])))

            @block.vector
            def _(dve):
                def ln_stats(key, st, src, waits):
                    def go(g, i):
                        for who, name in waits:
                            dve.wait_ge(*who.done(name, g))
                        for b in range(G):
                            last = nc.vector.bn_stats(stats[key][:, b, :], src[:, b, :])
                        last.then_inc(*st["dve"].mark(key + "stats"))
                        waits_apart(dve, prep, st["dve"].done(key + "stats", g))
                        for b in range(G):
                            last = nc.vector.bn_aggr(mv[key][:, b, :], stats[key][:, b, :])
                        last.then_inc(*st["dve"].mark(key + "aggr"))
                        dve.wait_ge(*st["dve"].done(key + "aggr", g))
                        for w in st["pool"].before(key + "pow", g):
                            dve.wait_ge(*w)
                        nc.vector.tensor_scalar(ve[key][:], mv[key][:, :, 1], EPS, None, ALU.add)\
                            .then_inc(*st["dve"].mark(key + "ve"))
                    return go

                def ln_apply(key, st, src, dst, frees, name=None):
                    def go(g, i):
                        for who, what in frees:
                            for w in who.before(what, g):
                                dve.wait_ge(*w)
                        dve.wait_ge(*st["pool"].done(key + "pow", g))
                        for b in range(G):
                            last = nc.vector.tensor_scalar(dst[:, b, :], src[:, b, :], mv[key][:, b, 0:1], rs[key][:, b:b + 1],
                                                           ALU.subtract, ALU.mult)
                        last.then_inc(*st["dve"].mark(name or key))
                    return go

                def scores(g, i, p, b, j):
                    st = steps[PASSES[p][1]]
                    n = TILES.index((p, b, j)) - TILES.index((p, 0, 0))
                    t, waits = probs.claim((p, b, j), i, st["pe"], "turn", UNITS[PASSES[p][1]], n)
                    bk = banks.of(("scores", p, b, j))[:, :].rearrange("p (h t) -> p h t", h=4)
                    m = mx[TILES.index((p, b, j)) % 2]
                    dve.wait_ge(*st["pe"].done("scores", g, n))
                    nc.vector.tensor_reduce(m[:], bk, AX, ALU.max).then_inc(*st["dve"].mark("max"))
                    for w in waits:
                        dve.wait_ge(*w)
                    dve.wait_ge(*st["dve"].done("max", g, n))
                    nc.vector.tensor_tensor(t[:], bk, m[:].unsqueeze(2).to_broadcast([128, 4, 128]), ALU.subtract)\
                        .then_inc(*st["dve"].mark("centre"))

                def back(p, b, unit):
                    def go(g, i):
                        st = steps[unit]
                        heads, hd, gw = PASSES[p][2:]
                        o = banks.of(("back", p, b))[:, :].rearrange("p (h c) -> p h c", c=gw)
                        r = recip[p]
                        dve.wait_ge(*st["pe"].done("back", g, b))
                        if b:
                            dve.wait_ge(*st["dve"].done("norm", g, b - 1))
                        else:
                            for w in st["dve"].before("norm", g):
                                dve.wait_ge(*w)
                        nc.vector.reciprocal(r[:, 0:heads], o[:, :, hd]).then_inc(*st["dve"].mark("recip"))
                        dve.wait_ge(*st["dve"].done("recip", g, b))
                        if p != "mix":
                            if p == "self":
                                dve.wait_ge(*self_in["dve"].done("keep", g))
                                keep = keep0[0]
                            else:
                                dve.wait_ge(*ctx_att["pool"].done("copies", g))
                                keep = keep1[1]
                            nc.vector.tensor_scalar(r[:, 0:heads], r[:, 0:heads], keep[:, b:b + 1], None, ALU.mult)\
                                .then_inc(*st["dve"].mark("rmask"))
                            dve.wait_ge(*st["dve"].done("rmask", g, b))
                        if b == 0:
                            free = {"self": (self_att["dve"], "ln1"), "ctx": (ctx_att["dve"], "ln2"),
                                    "mix": (mix_out["pe"], "attT")}[p]
                            for w in free[0].before(free[1], g):
                                dve.wait_ge(*w)
                        z = Z[p][:, b, :].rearrange("p (h c) -> p h c", c=hd)
                        nc.vector.tensor_tensor(z, o[:, :, 0:hd], r[:, 0:heads].unsqueeze(2).to_broadcast([128, heads, hd]),
                                                ALU.mult).then_inc(*st["dve"].mark("norm"))
                    return go

                def add_into(st, z, x, waits):
                    def go(g, i):
                        for who, name in waits:
                            dve.wait_ge(*who.done(name, g))
                        dve.wait_ge(*st["dve"].done("norm", g))
                        nc.vector.tensor_tensor(z[:], z[:], x[:], ALU.add).then_inc(*st["dve"].mark("add"))
                    return go

                def keep_rows(src, key, dst, st, waits, frees):
                    def go(g, i):
                        for who, name in waits:
                            dve.wait_ge(*(who.done(g) if name is None else who.done(name, g)))
                        for w in st["dve"].before("keep", g):
                            dve.wait_ge(*w)
                        nc.vector.tensor_reduce(amax[key][:], src[:], AX, ALU.max, apply_absolute_value=True)\
                            .then_inc(*st["dve"].mark("amax"))
                        dve.wait_ge(*st["dve"].done("amax", g))
                        for who, what in frees:
                            for w in who.before(what, g):
                                dve.wait_ge(*w)
                        nc.vector.tensor_scalar(dst[:], amax[key][:], 0.0, None, ALU.not_equal).then_inc(*st["dve"].mark("keep"))
                    return go

                def qkv(p, unit):
                    def go(g, i):
                        st = steps[unit]
                        for w in st["pe"].before("e0", g):
                            dve.wait_ge(*w)
                        dve.wait_ge(*st["act"].done("q", g))
                        q = QT[p][:].rearrange("p a (b s) -> p (a b) s", b=G)[:, :, 0:1]
                        nc.vector.tensor_tensor(q0[p][:], q.to_broadcast([128, DH * G, 8]),
                                                head_of[:].unsqueeze(1).to_broadcast([128, DH * G, 8]), ALU.mult)\
                            .then_inc(*st["dve"].mark("q0"))
                    return go

                def e0(p, unit):
                    def go(g, i):
                        st = steps[unit]
                        for w in st["pe"].before("len", g):
                            dve.wait_ge(*w)
                        dve.wait_ge(*st["pe"].done("e0", g))
                        nc.vector.tensor_scalar(nz[p][:], banks.of(("e0", p))[:, 0:G * L0_HEADS], 0.0, None, ALU.not_equal)\
                            .then_inc(*st["dve"].mark("nz"))
                    return go

                def length(p, unit, att):
                    def go(g, i):
                        st = steps[unit]
                        for w in st["dve"].before("vp", g):
                            dve.wait_ge(*w)
                        dve.wait_ge(*st["pe"].done("len", g))
                        nc.vector.tensor_scalar(valid[p][:], banks.of(("len", p))[:, 0:G * L0_HEADS], iota[:], None, ALU.is_gt)\
                            .then_inc(*st["dve"].mark("valid"))
                        dve.wait_ge(*st["dve"].done("valid", g))
                        dve.wait_ge(*st["act"].done("v", g))
                        for w in steps[att]["pe"].before("values", g):
                            dve.wait_ge(*w)
                        ok = valid[p][:].rearrange("p (b h) -> p b h", b=G)
                        nc.vector.tensor_copy(VP[p][:, :, :, L0_HD], ok)
                        for b in range(G):
                            last = nc.vector.tensor_tensor(VP[p][:, b, :, 0:L0_HD], VN[p][:, b, :].rearrange("p (h c) -> p h c", c=L0_HD),
                                                           ok[:, b, :].unsqueeze(2).to_broadcast([128, L0_HEADS, L0_HD]), ALU.mult)
                        last.then_inc(*st["dve"].mark("vp"))
                    return go

                def fc1(g, i):
                    for w in ffn["pe"].before("fc2", g):
                        dve.wait_ge(*w)
                    dve.wait_ge(*ffn["pe"].done("fc1", g))
                    for a in range(DH):
                        last = nc.vector.tensor_scalar(trn["HT"][:, a, :], banks.of(("fc1",))[:, a * W:(a + 1) * W],
                                                       cols["fc1_b"][:, a:a + 1], 0.0, ALU.add, ALU.max)
                    last.then_inc(*ffn["dve"].mark("relu"))

                def fc2(g, i):
                    for w in pair["dve"].before("lnF", g):
                        dve.wait_ge(*w)
                    for w in ffn["dve"].before("ln3", g):
                        dve.wait_ge(*w)
                    dve.wait_ge(*ffn["pe"].done("fc2", g))
                    nc.vector.tensor_tensor(nat["X3"][:], banks.of(("fc2",))[:, :].rearrange("p (b d) -> p b d", b=G),
                                            rows["fc2_b"][:].unsqueeze(1).to_broadcast([128, G, D]), ALU.add)\
                        .then_inc(*ffn["dve"].mark("bias"))
                    dve.wait_ge(*ffn["dve"].done("bias", g))
                    dve.wait_ge(*ffn["pool"].done("copies", g))
                    for b in range(G):
                        last = nc.vector.scalar_tensor_tensor(nat["X3"][:, b, :], nat["X3"][:, b, :], keep0[3][:, b:b + 1],
                                                              nat["X2"][:, b, :], ALU.mult, ALU.add)
                    last.then_inc(*ffn["dve"].mark("sum"))

                def CT(g, i):
                    dve.wait_ge(*pair["act"].done("HCT", g))
                    for w in pair["pe"].before("sc1", g):
                        dve.wait_ge(*w)
                    for a in range(DH):
                        last = nc.vector.tensor_scalar(trn["NXT"][:, a, :], banks.of(("CT",))[:, a * W:(a + 1) * W],
                                                       cols["n1_w"][:, a:a + 1], cols["n1_b"][:, a:a + 1], ALU.mult, ALU.add)
                    last.then_inc(*pair["dve"].mark("NXT"))

                def max_one(key, st, scale):
                    def go(g, i):
                        dve.wait_ge(*st["pe"].done("sc" + key, g))
                        for w in st["dve"].before("nm" + key, g):
                            dve.wait_ge(*w)
                        nc.vector.tensor_reduce(nmx[key][:], banks.of(("sc", key))[:, 0:W].rearrange("p (b t) -> p b t", b=G),
                                                AX, ALU.max).then_inc(*st["dve"].mark("mx" + key))
                        dve.wait_ge(*st["dve"].done("mx" + key, g))
                        for w in st["act"].before("exp" + key, g):
                            dve.wait_ge(*w)
                        nc.vector.tensor_scalar(nmax[key][:], nmx[key][:], -scale, None, ALU.mult)\
                            .then_inc(*st["dve"].mark("nm" + key))
                    return go

                def recip_one(key, st, g, users):
                    dve.wait_ge(*st["act"].done("exp" + key, g))
                    for w in st["dve"].before(users, g):
                        dve.wait_ge(*w)
                    nc.vector.reciprocal(rsum[key][:], psum_[key][:]).then_inc(*st["dve"].mark("rs" + key))
                    dve.wait_ge(*st["dve"].done("rs" + key, g))

                def av1(g, i):
                    recip_one("1", pair, g, "a4r")
                    dve.wait_ge(*pair["pe"].done("av1", g))
                    for w in pair["act"].before("gelu", g):
                        dve.wait_ge(*w)
                    nc.vector.tensor_tensor(a4[:], banks.of(("av1",))[:, 0:G * 4].rearrange("p (b c) -> p b c", b=G),
                                            rsum["1"][:].unsqueeze(2).to_broadcast([128, G, 4]), ALU.mult)\
                        .then_inc(*pair["dve"].mark("a4r"))
                    dve.wait_ge(*pair["dve"].done("a4r", g))
                    nc.vector.tensor_tensor(a4[:], a4[:], gate_b[:].unsqueeze(1).to_broadcast([128, G, 4]), ALU.add)\
                        .then_inc(*pair["dve"].mark("a4"))

                def av2(g, i):
                    recip_one("2", pair, g, "sa")
                    dve.wait_ge(*pair["pe"].done("av", g))
                    for w in real["pe"].before("x4T", g):
                        dve.wait_ge(*w)
                    for w in real["dve"].before("x5", g):
                        dve.wait_ge(*w)
                    for b in range(G):
                        last = nc.vector.scalar_tensor_tensor(nat["X4"][:, b, :], banks.of(("av", "2"))[:, b * D:(b + 1) * D],
                                                              rsum["2"][:, b:b + 1], rows["gam1"][:], ALU.mult, ALU.mult)
                    last.then_inc(*pair["dve"].mark("sa"))

                def av_real(g, i):
                    recip_one("real", real, g, "x5")
                    dve.wait_ge(*real["pe"].done("av", g))
                    for w in mix_out["dve"].before("res", g):
                        dve.wait_ge(*w)
                    for w in real["dve"].before("ln5", g):
                        dve.wait_ge(*w)
                    for b in range(G):
                        last = nc.vector.scalar_tensor_tensor(nat["X5"][:, b, :], banks.of(("av", "real"))[:, b * D:(b + 1) * D],
                                                              rsum["real"][:, b:b + 1], nat["X4"][:, b, :], ALU.mult, ALU.add)
                    last.then_inc(*real["dve"].mark("x5"))

                def kv3(g, i):
                    for w in mix_in["pe"].before("scores", g):
                        dve.wait_ge(*w)
                    dve.wait_ge(*mix_in["pe"].done("k", g))
                    for q in range(4):
                        r = slice(32 * q, 32 * q + 32)
                        last = nc.vector.tensor_tensor(kbd3[r, :, q, :], banks.of(("k3",))[r, :].rearrange("p (a w) -> p a w", a=DH),
                                                       cols["k3_b"][r, :].unsqueeze(2).to_broadcast([32, DH, W]), ALU.add)
                    last.then_inc(*mix_in["dve"].mark("k"))
                    for w in mix_in["pe"].before("values", g):
                        dve.wait_ge(*w)
                    dve.wait_ge(*mix_in["pe"].done("v", g))
                    for b in range(G):
                        last = nc.vector.tensor_tensor(vp3[:, b, :, 0:L3_HD],
                                                       banks.of(("v3",))[:, b * D:(b + 1) * D].rearrange("p (h c) -> p h c", c=L3_HD),
                                                       rows["v3_b"][:].rearrange("p (h c) -> p h c", c=L3_HD), ALU.add)
                    last.then_inc(*mix_in["dve"].mark("v"))

                def oproj(g, i):
                    for w in res_out.before(g):
                        dve.wait_ge(*w)
                    for w in mix_out["dve"].before("ln6", g):
                        dve.wait_ge(*w)
                    dve.wait_ge(*mix_out["pe"].done("o", g))
                    nc.vector.tensor_tensor(nat["X6"][:], banks.of(("o",))[:, :].rearrange("p (b d) -> p b d", b=G),
                                            rows["o_b"][:].unsqueeze(1).to_broadcast([128, G, D]), ALU.add)\
                        .then_inc(*mix_out["dve"].mark("obias"))
                    dve.wait_ge(*mix_out["dve"].done("obias", g))
                    nc.vector.tensor_tensor(nat["X6"][:], nat["X6"][:], nat["X5"][:], ALU.add).then_inc(*mix_out["dve"].mark("res"))

                def u(g, i):
                    for w in u_out.before(g):
                        dve.wait_ge(*w)
                    dve.wait_ge(*mix_out["pe"].done("u", g))
                    nc.vector.tensor_scalar(us[:].rearrange("p b s -> p (b s)"), banks.of(("u",))[0:NS, 0:W], u_b[:], None, ALU.add)\
                        .then_inc(*mix_out["dve"].mark("u"))

                def both(*fs):
                    def go(g, i):
                        for f in fs:
                            f(g, i)
                    return go

                drive(dve, [probs], dict(
                    scores=scores,
                    back_self0=back("self", 0, "self_att"), back_self1=back("self", 1, "self_att"),
                    back_ctx0=back("ctx", 0, "ctx_att"), back_ctx1=back("ctx", 1, "ctx_att"),
                    mix_norm0=back("mix", 0, "mix_out"), mix_norm1=back("mix", 1, "mix_out"),
                    keep_self=keep_rows(nat["X"], "self", keep0[0], self_in, [(x_in, None)],
                                 [(self_att["pool"], "keep"), (self_att["dve"], "rmask")]),
                    x1T=keep_rows(nat["X1"], "ctx", keep1[0], ctx_in, [(self_att["pool"], "ln1")],
                                  [(ctx_in["pool"], "mask"), (ctx_att["pool"], "copies")]),
                    qkv_self=qkv("self", "self_in"), qkv_ctx=qkv("ctx", "ctx_in"),
                    e0_self=e0("self", "self_in"), e0_ctx=e0("ctx", "ctx_in"),
                    len_self=length("self", "self_in", "self_att"), len_ctx=length("ctx", "ctx_in", "ctx_att"),
                    ln1a=both(lambda g, i: dve.wait_ge(*x_in2.done(g)), add_into(self_att, nat["Z1"], nat["XR"], []), ln_stats("ln1", self_att, nat["Z1"], [(self_att["dve"], "add")])),
                    ln1b=ln_apply("ln1", self_att, nat["Z1"], nat["X1"],
                                  [(ctx_in["pe"], "x1T"), (ctx_in["dve"], "amax"), (ctx_att["act"], "x1r")]),
                    ln2a=both(add_into(ctx_att, nat["Z2"], nat["X1r"], [(ctx_att["act"], "x1r")]),
                              ln_stats("ln2", ctx_att, nat["Z2"], [(ctx_att["dve"], "add")])),
                    ln2b=ln_apply("ln2", ctx_att, nat["Z2"], nat["X2"], [(ffn["pe"], "x2T"), (ffn["dve"], "sum")]),
                    fc1=fc1, fc2=fc2,
                    ln3a=ln_stats("ln3", ffn, nat["X3"], [(ffn["dve"], "sum")]),
                    ln3b=ln_apply("ln3", ffn, nat["X3"], nat["X3"], []),
                    lnFa=ln_stats("lnF", pair, nat["X3"], [(ffn["pool"], "ln3")]),
                    lnFb=ln_apply("lnF", pair, nat["X3"], nat["NF"], [(pair["pe"], "FT"), (pair["pool"], "x4")]),
                    lnCa=both(lambda g, i: dve.wait_ge(*ctx_in3.done(g)), ln_stats("lnC", pair, nat["CC"], [])),
                    lnCb=ln_apply("lnC", pair, nat["CC"], nat["HC"], [(pair["pe"], "CT")]),
                    CT=CT, sc1=max_one("1", pair, D ** -0.5), av1=av1,
                    cross=ln_stats("lnN", pair, nat["CR"], [(pair["act"], "cross")]),
                    lnNb=ln_apply("lnN", pair, nat["CR"], nat["NC"], [(pair["pe"], "ncT"), (pair["pe"], "av")]),
                    sc2=max_one("2", pair, D ** -0.5), av2=av2,
                    sc_real=max_one("real", real, 1.0), av_real=av_real,
                    ln5a=ln_stats("ln5", real, nat["X5"], [(real["dve"], "x5")]),
                    ln5b=ln_apply("ln5", real, nat["X5"], nat["H5"], [(real["pe"], "h5T")]),
                    kv3=kv3, oproj=oproj,
                    ln6a=ln_stats("ln6", mix_out, nat["X6"], [(mix_out["dve"], "res")]),
                    ln6b=ln_apply("ln6", mix_out, nat["X6"], nat["H6"], [(mix_out["pe"], "h6T")]),
                    u=u))

            @block.gpsimd
            def _(pool):
                def ln_pow(key, st):
                    def go(g, i):
                        name = {"lnN": "lnN"}.get(key, key)
                        for w in st["dve"].before({"ln1": "ln1", "ln2": "ln2"}.get(key, key), g):
                            pool.wait_ge(*w)
                        pool.wait_ge(*st["dve"].done(name + "ve", g))
                        nc.gpsimd.tensor_tensor(rs[key][:], ve[key][:], half[:], ALU.pow).then_inc(*st["pool"].mark(key + "pow"))
                    return go

                def ln_affine(key, st, dst, gain, shift):
                    def go(g, i):
                        pool.wait_ge(*st["dve"].done(key, g))
                        nc.gpsimd.tensor_tensor(dst[:], dst[:], rows[gain][:].unsqueeze(1).to_broadcast([128, G, D]), ALU.mult)\
                            .then_inc(*st["pool"].mark(key + "gain"))
                        pool.wait_ge(*st["pool"].done(key + "gain", g))
                        nc.gpsimd.tensor_tensor(dst[:], dst[:], rows[shift][:].unsqueeze(1).to_broadcast([128, G, D]), ALU.add)\
                            .then_inc(*st["pool"].mark(key))
                    return go

                def back_self1(g, i):
                    for w in ctx_att["pool"].before("copies", g):
                        pool.wait_ge(*w)
                    waits_apart(pool, prep, self_in["dve"].done("keep", g))
                    nc.gpsimd.tensor_scalar(keep0[1][:], keep0[0][:], 1.0, None, ALU.mult).then_inc(*self_att["pool"].mark("keep"))

                def copy1(g, i):
                    for w in ctx_att["dve"].before("rmask", g):
                        pool.wait_ge(*w)
                    for w in ffn["pool"].before("copies", g):
                        pool.wait_ge(*w)
                    waits_apart(pool, prep, self_att["pool"].done("keep", g), ctx_in["dve"].done("keep", g))
                    nc.gpsimd.tensor_scalar(keep1[1][:], keep1[0][:], 1.0, None, ALU.mult)
                    nc.gpsimd.tensor_scalar(keep0[2][:], keep0[1][:], 1.0, None, ALU.mult).then_inc(*ctx_att["pool"].mark("copies"))

                def x2T(g, i):
                    for w in ffn["dve"].before("sum", g):
                        pool.wait_ge(*w)
                    waits_apart(pool, prep, ctx_att["pool"].done("copies", g))
                    nc.gpsimd.tensor_scalar(keep0[3][:], keep0[2][:], 1.0, None, ALU.mult).then_inc(*ffn["pool"].mark("copies"))

                def x1T(g, i):
                    waits_apart(pool, prep, ctx_in2.done(g), ctx_in["dve"].done("keep", g))
                    for b in range(G):
                        last = nc.gpsimd.tensor_scalar(nat["CB"][:, b, :], nat["CB"][:, b, :], keep1[0][:, b:b + 1], None, ALU.mult)
                    last.then_inc(*ctx_in["pool"].mark("mask"))

                def kbd(p, unit, att):
                    def go(g, i):
                        st = steps[unit]
                        waits_apart(pool, prep, *steps[att]["pe"].before("scores", g), st["act"].done("k", g))
                        for h in range(8):
                            last = nc.gpsimd.tensor_scalar(KBD[p][:, :, h, :], KT[p][:], head_of[:, h:h + 1], None, ALU.mult)
                        last.then_inc(*st["pool"].mark("kbd"))
                    return go

                def av2(g, i):
                    pool.wait_ge(*pair["dve"].done("sa", g))
                    nc.gpsimd.tensor_tensor(nat["X4"][:], nat["X4"][:], nat["CR"][:], ALU.add).then_inc(*pair["pool"].mark("skip"))
                    pool.wait_ge(*pair["pool"].done("skip", g))
                    nc.gpsimd.tensor_tensor(nat["X4"][:], nat["X4"][:], rows["gam2"][:].unsqueeze(1).to_broadcast([128, G, D]), ALU.mult)\
                        .then_inc(*pair["pool"].mark("gam2"))
                    pool.wait_ge(*pair["pool"].done("gam2", g))
                    nc.gpsimd.tensor_tensor(nat["X4"][:], nat["X4"][:], nat["NF"][:], ALU.add).then_inc(*pair["pool"].mark("x4"))

                drive(pool, [], dict(
                    back_self1=back_self1,
                    ln1a=ln_pow("ln1", self_att), ln1b=ln_affine("ln1", self_att, nat["X1"], "ln1_g", "ln1_b"),
                    copy1=copy1, x2T=x2T, x1T=x1T,
                    ln2a=ln_pow("ln2", ctx_att), ln2b=ln_affine("ln2", ctx_att, nat["X2"], "ln2_g", "ln2_b"),
                    ln3a=ln_pow("ln3", ffn), ln3b=ln_affine("ln3", ffn, nat["X3"], "ln3_g", "ln3_b"),
                    lnFa=ln_pow("lnF", pair), lnFb=ln_affine("lnF", pair, nat["NF"], "n2_w", "n2_b"),
                    lnCa=ln_pow("lnC", pair), cross=ln_pow("lnN", pair),
                    lnNb=ln_affine("lnN", pair, nat["NC"], "n3_w", "n3_b"),
                    ln5a=ln_pow("ln5", real), ln6a=ln_pow("ln6", mix_out),
                    kbd_self=kbd("self", "self_in", "self_att"), kbd_ctx=kbd("ctx", "ctx_in", "ctx_att"),
                    av2=av2))

        HB = B // 2
        NB = 4
        CHUNKS = S // TC
        u_all = kbd12[:].rearrange("p k a h w -> p (k a h w)").rearrange("p (b t) -> p b t", t=S)
        a2 = nat["X"][:, 0, 0:128]
        c2 = nat["CB"][:, 0, :]
        gbuf = [nat["Z1"][:, n // 2, (n % 2) * HB:(n % 2) * HB + HB] for n in range(4)]
        sblk = [nat["Z2"][:, n, 0:128] for n in range(2)]
        res_t = [trn_all[:, 4 * n:4 * n + 4, :, :].rearrange("p k a w -> p (k a w)").rearrange("p (t d) -> p t d", d=D)
                 for n in range(NB)]
        vbank, obank = pbank[0:2], pbank[2:4]

        started, scan_in, m_ready, v_ready, g_ready, s_ready, o_ready, out_ready = (
            sem(n) for n in ("started", "scan_in", "m_ready", "v_ready", "g_ready", "s_ready", "o_ready", "out_ready"))
        res_in = [sem(f"res_in{n}") for n in range(NB)]
        chunk_out = [sem(f"chunk_out{n}") for n in range(NB)]

        with nc.Block() as block:
            @block.vector
            def _(dve):
                nc.vector.memset(nat["X"][:], 0.0)
                nc.vector.memset(nat["Z1"][:], 0.0)
                nc.vector.memset(nat["Z2"][:], 0.0).then_inc(started, 1)
                dve.wait_ge(started, 1)

            @block.sync
            def _(sp):
                sp.wait_ge(started, 1)
                for k in range(2):
                    r = slice(NS * k, NS * k + NS)
                    sp.dma_start(nat["X"][r, 0, NS * k:NS * k + NS], dram["a_t"]).then_inc(scan_in, 16)
                    sp.dma_start(nat["CB"][r, 0, :], dram["c_mat"]).then_inc(scan_in, 16)
                    sp.dma_start(u_all[r, :, :], u_d[k * HB:(k + 1) * HB].rearrange("b n s -> n b s")).then_inc(scan_in, 16)
                sp.wait_ge(scan_in, 96)

        with nc.Block() as block:
            def chunks(eng, body):
                for c in range(NB):
                    body(c, c, 0)
                with eng.Fori(1, CHUNKS // NB) as h:
                    for k in range(NB):
                        body(NB * h + k, k, h)

            def at_least(n, low):
                return not isinstance(n, int) or n >= low

            @block.sync
            def _(sp):
                def load(c, k):
                    sp.dma_start(res_t[k], res_d[:, bass.ds(c * TC, TC), :]).then_inc(res_in[k], 16)

                def store(c, k):
                    sp.wait_ge(out_ready, (c + 1) * TC)
                    sp.dma_start(out_d[:, bass.ds(c * TC, TC), :], res_t[k]).then_inc(chunk_out[k], 16)

                load(0, 0)
                load(1, 1)
                for c in range(2):
                    load(c + 2, c + 2)
                    store(c, c)
                with sp.Fori(0, CHUNKS // NB - 1) as h:
                    for k in range(NB):
                        c = NB * h + k + 2
                        sp.wait_ge(chunk_out[k], 16 * (h + 1))
                        load(c + 2, k)
                        store(c, (k + 2) % NB)
                for c in range(CHUNKS - 2, CHUNKS):
                    store(c, c % NB)
                for k in range(NB):
                    sp.wait_ge(chunk_out[k], 16 * (CHUNKS // NB))

            @block.gpsimd
            def _(pool):
                def body(c, k, r):
                    pool.wait_ge(res_in[k], 16 * (r + 1))
                    nc.gpsimd.tensor_tensor(res_t[k], res_t[k], mod[:].unsqueeze(1).to_broadcast([128, TC, D]), ALU.add)\
                        .then_inc(m_ready, 1)

                chunks(pool, body)

            @block.tensor
            def _(pe):
                def output(n, k):
                    pe.wait_ge(s_ready, n + 1)
                    if at_least(n, 2):
                        pe.wait_ge(out_ready, n - 1)
                    nc.tensor.matmul(obank[k][:, 0:D], sblk[k], c2, start=True, stop=True).then_inc(o_ready, 1)

                def body(c, k, _):
                    for t in range(TC):
                        n = c * TC + t
                        if not at_least(n, 1):
                            continue
                        v = vbank[t % 2]
                        if at_least(n, 3):
                            pe.wait_ge(g_ready, n - 2)
                        nc.tensor.matmul(v[:, 0:HB], a2, u_all[:, :, bass.ds(n - 1, 1)], start=True, stop=False)
                        if at_least(n, 2):
                            pe.wait_ge(g_ready, n - 1)
                        nc.tensor.matmul(v[:, 0:HB], a2, gbuf[(t - 1) % 4], start=False, stop=True).then_inc(v_ready, 1)
                        output(n - 1, (t - 1) % 2)

                chunks(pe, body)
                output(S - 1, (S - 1) % 2)

            @block.scalar
            def _(act):
                def body(c, k, _):
                    for t in range(TC):
                        n = c * TC + t
                        if not at_least(n, 1):
                            continue
                        if at_least(n, 4):
                            act.wait_ge(s_ready, n - 3)
                        act.wait_ge(v_ready, n)
                        nc.scalar.activation(gbuf[t % 4], vbank[t % 2][:, 0:HB], ACT.Silu).then_inc(g_ready, 1)

                chunks(act, body)

            @block.vector
            def _(dve):
                def add(n, k, kb, t):
                    dve.wait_ge(o_ready, n + 1)
                    nc.vector.tensor_tensor(res_t[kb][:, t, :], res_t[kb][:, t, :], obank[k][:, 0:D], ALU.add).then_inc(out_ready, 1)

                def body(c, k, _):
                    for t in range(TC):
                        n = c * TC + t
                        if at_least(n, 1):
                            dve.wait_ge(g_ready, n)
                        if at_least(n, 2):
                            dve.wait_ge(o_ready, n - 1)
                        for half_ in range(2):
                            r = slice(NS * half_, NS * half_ + NS)
                            last = nc.vector.tensor_tensor(sblk[t % 2][r, half_ * HB:(half_ + 1) * HB], gbuf[t % 4][r, :],
                                                           u_all[r, :, bass.ds(n, 1)].rearrange("p b t -> p (b t)"), ALU.add)
                        last.then_inc(s_ready, 1)
                        if t == 1:
                            dve.wait_ge(m_ready, c + 1)
                        if at_least(n, 1):
                            add(n - 1, (t - 1) % 2, k if t else (k - 1) % NB, (t - 1) % TC)

                chunks(dve, body)
                add(S - 1, (S - 1) % 2, (CHUNKS - 1) % NB, TC - 1)


def layouts(inputs):
    f = {k: np.asarray(v) for k, v in inputs.items()}
    c = np.ascontiguousarray

    def heads(w):
        return c(w.transpose(1, 0, 2).reshape(D, D))

    qkv, qkv_b = f["L3_xattn_W_qkv"], f["L3_xattn_b_qkv"]
    a = {"x": f["x"], "ctx": f["ctx_1024"], "ctxb": f["ctxb_2048x64"]}
    for n in ("q1", "k1", "v1", "q2", "k2", "v2"):
        a["w_" + n] = heads(f["L0_xattn_W" + n])
    for n in ("fc1", "fc2"):
        a["w_" + n] = c(f[f"L0_xattn_{n}_w"].T)
    for k, n in enumerate(("q3", "k3", "v3")):
        a["w_" + n] = c(qkv[k * D:(k + 1) * D].T)
    a["w_o3"] = c(f["L3_xattn_W_o"].T)
    a["w_gate"] = c(f["L1_xattn_fc1_w"].T)
    a["w_cross"] = np.concatenate([f["L1_xattn_fc2_w"].T, f["L1_xattn_fc2_b"][None]], 0)
    a["w_in"], a["b_mat"], a["c_mat"] = f["L3_xattn_W_in"], f["L3_xattn_Bmat"], f["L3_xattn_Cmat"]
    a["w_prog"], a["a_t"] = c(f["L3_xattn_W_prog"].T), c(f["L3_xattn_A"].T)
    a["gate_b"], a["prog_b"] = f["L1_xattn_fc1_b"], f["L3_xattn_b_prog"]
    for n in ("ln1", "ln2", "ln3"):
        for e in ("g", "b"):
            a[f"row_{n}_{e}"] = f[f"L0_xattn_{n}_{e}"]
    for k in ("2", "3"):
        for e in ("w", "b"):
            a[f"row_n{k}_{e}"] = f[f"L1_xattn_norm{k}_{e}"]
    a["row_gam1"], a["row_gam2"] = f["L1_xattn_gamma1"], f["L1_xattn_gamma2"]
    a["row_fc2_b"], a["row_o_b"], a["row_v3_b"] = f["L0_xattn_fc2_b"], f["L3_xattn_b_o"], qkv_b[2 * D:]
    a["col_n1_w"], a["col_n1_b"] = f["L1_xattn_norm1_w"], f["L1_xattn_norm1_b"]
    a["col_g1"], a["col_be1"] = f["L3_xattn_g1"], f["L3_xattn_beta1"]
    a["col_g2"], a["col_be2"] = f["L3_xattn_g2"], f["L3_xattn_beta2"]
    a["col_fc1_b"], a["col_q3_b"], a["col_k3_b"] = f["L0_xattn_fc1_b"], qkv_b[0:D], qkv_b[D:2 * D]
    a["col_in_b"] = f["L3_xattn_b_in"]
    p = np.arange(128)
    a["ident"] = np.eye(128, dtype=np.float32)
    a["head_of"] = (p[:, None] // L0_HD == np.arange(8)[None]).astype(np.float32)
    a["iota"] = p[:, None].astype(np.float32)
    a["causal"] = (p[None, :] > p[:, None]).astype(np.float32)
    return {k: c(v.reshape(DH, 128).T if k.startswith("col_") else v) for k, v in a.items()}


def kernel(**inputs):
    import concourse.bacc as bacc
    from concourse.bass_utils import run_bass_kernel_spmd

    arrays = layouts(inputs)
    nc = bacc.Bacc("TRN2", target_bir_lowering=False, num_devices=1)
    dram = {n: nc.dram_tensor("in_" + n, a.shape, F32, kind="ExternalInput").ap() for n, a in arrays.items()}
    dram["res"] = nc.dram_tensor("residual", (B, S, D), F32, kind="Internal").ap()
    dram["u"] = nc.dram_tensor("u_turned", (B, NS, S), F32, kind="Internal").ap()
    dram["out"] = nc.dram_tensor("out", (B, S, D), F32, kind="ExternalOutput").ap()
    build(nc, dram)
    r = run_bass_kernel_spmd(nc, [{"in_" + n: a for n, a in arrays.items()}], core_ids=[0])
    return r.results[0]["out"]
```
